# Optimizing a Trainium2 kernel written in Bass

```python
import numpy as np
import jax
import jax.numpy as jnp

def _softmax(x, axis=-1):
    return jax.nn.softmax(x, axis=axis)

def _gelu(x):
    return jax.nn.gelu(x, approximate=True)

def _silu(x):
    return jax.nn.silu(x)

def _sigmoid(x):
    return jax.nn.sigmoid(x)

def _layernorm(x, axis=-1, eps=1e-05):
    m = jnp.mean(x, axis=axis, keepdims=True)
    v = jnp.var(x, axis=axis, keepdims=True)
    return (x - m) / jnp.sqrt(v + eps)

def _scatter_add(tgt, idx, src, axis=0):
    return tgt.at[idx].add(src)

def _segment_sum(src, seg, n):
    return jax.ops.segment_sum(src, seg, n)
kernel_name = 'mk_gnn_preln_d1_gnn_r8_da9ec8'

def setup_inputs(seed: int=0):
    np.random.seed(seed)
    _w = jnp.asarray

    def _rec_inputs():
        import jax
        import jax.numpy as jnp
        _gk = jax.random.key(seed)
        x = -6.415e-05 + 1 * jax.random.normal(jax.random.fold_in(_gk, 1), (1250, 1024), jnp.float32)
        src = jax.random.randint(jax.random.fold_in(_gk, 2), (40000,), 0, 1250, jnp.int32)
        dst = jax.random.randint(jax.random.fold_in(_gk, 3), (40000,), 0, 1250, jnp.int32)
        _o = jnp.argsort(dst, stable=True)
        src = src[_o]
        dst = dst[_o]
        return (x, src, dst)
    x, src, dst = _rec_inputs()

    def _L0_gnn_setup():
        import jax, jax.numpy as jnp
        import numpy as np
        N_NODES = 1250
        N_EDGES = 10000
        D = 1024

        def _sage_sum(h, src, dst, Ws, Wn, b):
            h_neigh = jax.ops.segment_sum(h[src], dst, num_segments=N_NODES)
            return h @ Ws + h_neigh @ Wn + b
        key = jax.random.key(seed)
        ks = jax.random.split(key, 8)
        s = 1.0 / np.sqrt(D)
        x = jax.random.normal(ks[0], (N_NODES, D), dtype=jnp.float32)
        edge_index = jax.random.randint(ks[1], (2, N_EDGES), 0, N_NODES, dtype=jnp.int32)
        Ws1 = jax.random.normal(ks[2], (D, D), dtype=jnp.float32) * s
        Wn1 = jax.random.normal(ks[3], (D, D), dtype=jnp.float32) * s
        b1 = jnp.zeros((D,), dtype=jnp.float32)
        Ws2 = jax.random.normal(ks[4], (D, D), dtype=jnp.float32) * s
        Wn2 = jax.random.normal(ks[5], (D, D), dtype=jnp.float32) * s
        b2 = jnp.zeros((D,), dtype=jnp.float32)
        return {'x': x, 'edge_index': edge_index, 'Ws1': Ws1, 'Wn1': Wn1, 'b1': b1, 'Ws2': Ws2, 'Wn2': Wn2, 'b2': b2}
    _L0_gnn_all = _L0_gnn_setup()
    _L0_gnn_in = {k: v for k, v in _L0_gnn_all.items() if k in ('Ws1', 'Wn1', 'b1', 'Ws2', 'Wn2', 'b2')}
    del _L0_gnn_all
    return {'x': x, 'src': src, 'dst': dst, 'L0_gnn_Ws1': _L0_gnn_in['Ws1'], 'L0_gnn_Wn1': _L0_gnn_in['Wn1'], 'L0_gnn_b1': _L0_gnn_in['b1'], 'L0_gnn_Ws2': _L0_gnn_in['Ws2'], 'L0_gnn_Wn2': _L0_gnn_in['Wn2'], 'L0_gnn_b2': _L0_gnn_in['b2']}

def reference(x, src, dst, L0_gnn_Ws1, L0_gnn_Wn1, L0_gnn_b1, L0_gnn_Ws2, L0_gnn_Wn2, L0_gnn_b2):
    import jax
    import jax.numpy as jnp

    def _L0_gnn_ref(x, edge_index, Ws1, Wn1, b1, Ws2, Wn2, b2):
        import jax, jax.numpy as jnp
        import numpy as np
        N_NODES = 1250
        N_EDGES = 10000
        D = 1024

        def _sage_sum(h, src, dst, Ws, Wn, b):
            h_neigh = jax.ops.segment_sum(h[src], dst, num_segments=N_NODES)
            return h @ Ws + h_neigh @ Wn + b
        src, dst = (edge_index[0], edge_index[1])
        h = _sage_sum(x, src, dst, Ws1, Wn1, b1)
        h = _sage_sum(h, src, dst, Ws2, Wn2, b2)
        return h
    edge_index = jnp.stack([src, dst])
    h = jnp.maximum(_layernorm(x, axis=-1), 0.0)
    x = x + _L0_gnn_ref(h, edge_index, L0_gnn_Ws1, L0_gnn_Wn1, L0_gnn_b1, L0_gnn_Ws2, L0_gnn_Wn2, L0_gnn_b2)
    return x

_drawn_inputs = setup_inputs


def setup_inputs(seed=0):
    import zlib

    import numpy as np

    out = dict(_drawn_inputs(seed))
    spreads = {'L0_gnn_b1': (0.0, 0.8), 'L0_gnn_b2': (0.0, 0.8)}
    factors = {}
    for name, (base, spread) in spreads.items():
        noise = np.random.default_rng([zlib.crc32(name.encode()), seed]).standard_normal(out[name].shape)
        drawn = base * np.exp(spread * noise) if base else spread * noise
        out[name] = jnp.asarray(drawn.astype(out[name].dtype))
    for name, factor in factors.items():
        out[name] = (out[name] * factor).astype(out[name].dtype)
    return out
```

```python
from contextlib import ExitStack

import concourse.bass as bass
from concourse import mybir

ALU = mybir.AluOpType
ACT = mybir.ActivationFunctionType
AX_X = mybir.AxisListType.X
F32 = mybir.dt.float32
F32R = mybir.dt.float32r
F16 = mybir.dt.float16
BF16 = mybir.dt.bfloat16
I32 = mybir.dt.int32
U32 = mybir.dt.uint32
U16 = mybir.dt.uint16

P = 128
EPS = 1e-5
ROUND = float(3 * 2 ** 22)


def gnn_program(nc, x, src, dst, Ws, Wn, b, out):
    N, D = x.shape
    E = src.shape[0]
    MT = 10
    Q = N // MT
    KT = D // P
    CH = 2
    CW = D // CH
    KC = CW // P
    EP = 125
    EJ = 8
    GE = EP * EJ
    NG = E // GE
    WIN_D = 40
    WIN = WIN_D * MT
    GPT = NG // MT
    EXACT = 4096
    assert N == MT * Q and NG * GE == E and NG % MT == 0 and WIN <= 512 and Q <= P and MT % 2 == 0

    x_rows = x.rearrange("(q m) d -> q (m d)", m=MT)
    x_tiles = x.rearrange("(q m) d -> m q d", m=MT)
    out_tiles = out.rearrange("(q m) d -> m q d", m=MT)
    w_tiles = [[W.rearrange("(t p) n -> p t n", p=P) for W in pair] for pair in zip(Wn, Ws)]
    h1_spill = nc.dram_tensor("h1_spill", [MT, P, KC * Q], F32).ap()

    phases = [(l, c, odd) for l in range(2) for c in range(CH) for odd in range(2)]
    XP = MT // 2

    with ExitStack() as ctx:
        def sb(name, shape, dt):
            return ctx.enter_context(nc.sbuf_tensor(name, shape, dt))

        def psum(name, shape, dt=F32):
            return ctx.enter_context(nc.psum_tensor(name, shape, dt))

        def sem(name):
            return ctx.enter_context(nc.semaphore(name))

        hT = sb("hT", [P, MT, KT, Q], F32)
        lhs_hi = sb("lhs_hi", [P, 2, KT, Q], F32R)
        lhs_lo = sb("lhs_lo", [P, 2, KT, Q], F32R)
        AT = sb("AT", [Q, N * MT + WIN], U16)
        w_raw = sb("w_raw", [P, 2, CW], F32)
        wn_hi = sb("wn_hi", [P, KT, CW], F32R)
        wn_lo = sb("wn_lo", [P, KT, CW], F32R)
        bias = sb("bias", [Q, D], F32)
        ident = sb("ident", [P, P], F32)
        iota_w = sb("iota_w", [EP, WIN], F16)
        iota_q = sb("iota_q", [EP, Q], F32)
        key_t = sb("key_t", [EP, NG, EJ], F32)
        negq_t = sb("negq_t", [EP, NG, EJ], F32)
        stats = sb("stats", [Q, MT, 2, 6], F32)
        mean_var = sb("mean_var", [Q, MT, 2], F32)
        rstd = sb("rstd", [Q, MT], F32)
        group_col = sb("group_col", [NG, 8], F32)
        start_row = sb("start_row", [1, NG], F32)
        start_int = sb("start_int", [1, NG], I32)
        row_f = sb("row_f", [1, 4], F32)
        passes_int = sb("passes_int", [1, 1], I32)

        with ExitStack() as early:
            def early_sb(name, shape, dt):
                return early.enter_context(nc.sbuf_tensor(name, shape, dt))

            x_all = early_sb("x_all", [Q, MT, D], F32)
            dst_i = early_sb("dst_i", [NG, GE], I32)
            src_i = early_sb("src_i", [NG, GE], I32)
            dst_f = early_sb("dst_f", [NG, GE], F32)
            src_f = early_sb("src_f", [NG, GE], F32)
            negq = early_sb("negq", [NG, GE], F32)
            key = early_sb("key", [NG, GE], F32)
        p_hi = sb("p_hi", [Q, MT, CW], F32R)
        p_lo = sb("p_lo", [Q, MT, CW], F32R)
        ws_hi = sb("ws_hi", [P, KT, CW], F32R)
        ws_lo = sb("ws_lo", [P, KT, CW], F32R)
        with ExitStack() as early:
            def early_sb(name, shape, dt):
                return early.enter_context(nc.sbuf_tensor(name, shape, dt))

            dst_hot = early_sb("dst_hot", [EP, 2, EJ, WIN], BF16)
            src_sq = early_sb("src_sq", [EP, 2, EJ, Q], BF16)
            src_hot = early_sb("src_hot", [EP, 2, EJ, Q], BF16)
        a_hi = sb("a_hi", [Q, 2, MT, Q], F32R)
        tile_out = sb("tile_out", [Q, 2, CW], F32)
        side = sb("side", [P, 2, CW], F32)

        w_hi, w_lo = [wn_hi, ws_hi], [wn_lo, ws_lo]

        acc = [psum(f"acc{s}", [Q, CW]) for s in range(2)]
        win = [psum(f"win{s}", [Q, 512]) for s in range(2)]
        tp = [psum(f"tp{s}", [P, 512]) for s in range(2)]
        kp = [psum(f"kp{s}", [P, 512]) for s in range(2)]

        edges_loaded = sem("edges_loaded")
        x_loaded = [sem(f"x_loaded{i}") for i in range(XP)]
        bias_loaded = sem("bias_loaded")
        w_raw_loaded = [sem(f"w_raw_loaded{s}") for s in range(2)]
        w_hi_ready = sem("w_hi_ready")
        w_lo_ready = sem("w_lo_ready")
        consts_ready = sem("consts_ready")
        vec_step = sem("vec_step")
        group_ready = sem("group_ready")
        key_cols_ready = sem("key_cols_ready")
        keys_turned = sem("keys_turned")
        keys_ready = sem("keys_ready")
        var_ready = sem("var_ready")
        std_ready = sem("std_ready")
        xn_ready = sem("xn_ready")
        xt_ready = sem("xt_ready")
        ht_ready = sem("ht_ready")
        src_sq_ready = sem("src_sq_ready")
        src_hot_ready = sem("src_hot_ready")
        dst_hot_ready = sem("dst_hot_ready")
        win_ready = sem("win_ready")
        win_added = sem("win_added")
        pass_keys = sem("pass_keys")
        a_ready = sem("a_ready")
        lhs_hi_ready = sem("lhs_hi_ready")
        lhs_lo_ready = sem("lhs_lo_ready")
        tile_done = sem("tile_done")
        p_hi_ready = sem("p_hi_ready")
        p_lo_ready = sem("p_lo_ready")
        a_hi_ready = sem("a_hi_ready")
        out_ready = sem("out_ready")
        h1t_turned = sem("h1t_turned")
        h1t_ready = sem("h1t_ready")
        spilled = [sem(f"spilled{s}") for s in range(2)]
        reloaded = sem("reloaded")
        xres_loaded = [sem(f"xres_loaded{s}") for s in range(2)]
        xres_ready = sem("xres_ready")
        stored = [sem(f"stored{s}") for s in range(2)]

        def wait(eng, s, count):
            if not isinstance(count, int) or count > 0:
                eng.wait_ge(s, count)

        def pairs(eng, body, first=0, last=MT // 2):
            body(first)
            with eng.Fori(first + 1, last) as i:
                body(i)

        block = ctx.enter_context(nc.Block())

        @block.sync
        def _(sp):
            def load_w(f, t, s):
                l, c, odd = phases[f]
                wait(sp, w_hi_ready, KT * f + t - 1)
                wait(sp, w_lo_ready, KT * f + t - 1)
                sp.dma_start(w_raw[:, s, :], w_tiles[l][odd][:, t, c * CW:(c + 1) * CW]).then_inc(w_raw_loaded[s], 16)

            sp.dma_start(dst_i[:], dst.rearrange("(g e) -> g e", g=NG)).then_inc(edges_loaded, 16)
            sp.dma_start(src_i[:], src.rearrange("(g e) -> g e", g=NG)).then_inc(edges_loaded, 16)
            for i in range(XP):
                sp.dma_start(x_all[:, 2 * i:2 * i + 2, :], x_rows[:, 2 * i * D:(2 * i + 2) * D]).then_inc(x_loaded[i], 16)
            sp.dma_start(bias[:], b[0].partition_broadcast(Q)).then_inc(bias_loaded, 16)
            for t in range(KT):
                load_w(0, t, t % 2)

            for f, (l, c, odd) in enumerate(phases):
                chunk = slice(c * CW, (c + 1) * CW)
                k = CH * l + c
                if l == 1 and c == 0 and odd == 0:
                    sp.wait_ge(out_ready, MT * CH)
                    sp.dma_start(bias[:], b[1].partition_broadcast(Q)).then_inc(bias_loaded, 16)
                if l == 1 and odd == 1:
                    for s in range(2):
                        wait(sp, out_ready, MT * k)
                        sp.dma_start(side[0:Q, s, :], x_tiles[s][:, chunk]).then_inc(xres_loaded[s], 16)

                def pair(i, last=False):
                    if f + 1 < len(phases) and not last:
                        for s in range(2):
                            load_w(f + 1, 2 * i + s, s)
                    if not odd:
                        return
                    for s in range(2):
                        m = 2 * i + s
                        if l == 0 and c == 0:
                            sp.wait_ge(h1t_ready, m + 1)
                            sp.dma_start(h1_spill[m], side[:, s, 0:KC * Q]).then_inc(spilled[s], 16)
                        if l == 0 and c == 1:
                            sp.wait_ge(lhs_hi_ready, MT * f + m + 1)
                            sp.wait_ge(lhs_lo_ready, MT * f + m + 1)
                            sp.dma_start(hT[:, m, 0:KC, :], h1_spill[m].rearrange("p (t q) -> p t q", q=Q))\
                              .then_inc(reloaded, 16)
                        if l == 1:
                            sp.wait_ge(out_ready, MT * k + m + 1)
                            sp.dma_start(out_tiles[m][:, chunk], tile_out[:, s, :]).then_inc(stored[s], 16)
                            if not last:
                                sp.dma_start(side[0:Q, s, :], x_tiles[m + 2][:, chunk]).then_inc(xres_loaded[s], 16)

                if l == 0 and c == 1 and odd == 1:
                    for s in range(2):
                        sp.wait_ge(spilled[s], 16 * (MT // 2))
                if odd or f + 1 < len(phases):
                    pairs(sp, pair, 0, MT // 2 - 1)
                    pair(MT // 2 - 1, last=True)
            for s in range(2):
                sp.wait_ge(stored[s], 16 * CH * (MT // 2))

        def split_w_lo(eng, f, n, s):
            t = 2 * n + s
            eng.wait_ge(w_hi_ready, KT * f + t + 1)
            eng.tensor_tensor(w_lo[f % 2][:, t, :], w_raw[:, s, :], w_hi[f % 2][:, t, :].bitcast(F32),
                              ALU.subtract).then_inc(w_lo_ready, 1)

        def stage_lo(eng, u, m, s):
            eng.wait_ge(lhs_hi_ready, u + 1)
            eng.tensor_tensor(lhs_lo[:, s], hT[:, m], lhs_hi[:, s].bitcast(F32),
                              ALU.subtract).then_inc(lhs_lo_ready, 1)

        @block.gpsimd
        def _(pool):
            pool.memset(ident[:], 0.0).then_inc(consts_ready, 1)
            pool.wait_ge(consts_ready, 1)
            pool.affine_select(out=ident[:], in_=ident[:], compare_op=ALU.not_equal, fill=1.0, base=0,
                               pattern=[[-1, P]], channel_multiplier=1).then_inc(consts_ready, 1)
            pool.iota(iota_q[:], [[1, Q]], base=0, channel_multiplier=0,
                      allow_small_or_imprecise_dtypes=True).then_inc(consts_ready, 1)
            pool.iota(iota_w[:], [[1, WIN]], base=0, channel_multiplier=0,
                      allow_small_or_imprecise_dtypes=True).then_inc(consts_ready, 1)
            pool.memset(AT[:].bitcast(U32), 0).then_inc(consts_ready, 1)

            for t in range(KT):
                split_w_lo(pool, 0, t // 2, t % 2)
            stage_lo(pool, 0, 0, 0)

            def pair(i, last=False):
                for s in range(2):
                    m = 2 * i + s
                    stage_lo(pool, m + 1, 0 if last and s == 1 else m + 1, 1 - s)
                    if not (isinstance(i, int) and i == 0):
                        split_w_lo(pool, 1, i - 1, s)

            pairs(pool, pair, 0, MT // 2 - 1)
            pair(MT // 2 - 1, last=True)

            pool.wait_ge(bias_loaded, 32)
            for c in range(CH):
                def add_bias(i):
                    for s in range(2):
                        pool.wait_ge(xres_loaded[s], 16 * (c * (MT // 2) + i + 1))
                        pool.tensor_tensor(side[0:Q, s, :], side[0:Q, s, :], bias[:, c * CW:(c + 1) * CW],
                                           ALU.add).then_inc(xres_ready, 1)

                pairs(pool, add_bias)

        @block.scalar
        def _(act):
            def split_w_hi(f, n, s):
                act.wait_ge(w_raw_loaded[s], 16 * (KT // 2 * f + n + 1))
                act.activation(w_hi[f % 2][:, 2 * n + s, :], w_raw[:, s, :], ACT.Copy).then_inc(w_hi_ready, 1)

            def stage_hi(u, m, s):
                wait(act, tile_done, u - 1)
                act.activation(lhs_hi[:, s], hT[:, m], ACT.Copy).then_inc(lhs_hi_ready, 1)

            def stage_a(n, u, m, s):
                wait(act, tile_done, u - 1)
                view = AT[:, 0:N * MT].rearrange("p (q m c) -> p m c q", m=MT, c=MT)
                act.activation(a_hi[:, s], view[:, m], ACT.Copy).then_inc(a_hi_ready, 1)

            def evacuate_p(n, m, s):
                act.activation(p_hi[:, m, :], acc[s][:], ACT.Copy).then_inc(p_hi_ready, 1)

            def source_hots(n, g, s):
                wait(act, src_hot_ready, n - 1)
                for j in range(EJ):
                    square = act.activation(src_sq[:, s, j, :], iota_q[:], ACT.Square, bias=negq_t[:, g, j:j + 1])
                square.then_inc(src_sq_ready, 1)
                act.wait_ge(src_sq_ready, n + 1)
                wait(act, win_ready, n - 1)
                act.activation(src_hot[:, s], src_sq[:, s], ACT.Relu, bias=1.0, scale=-1.0).then_inc(src_hot_ready, 1)

            act.wait_ge(var_ready, 1)
            act.activation(rstd[:], rstd[:], ACT.Sqrt).then_inc(std_ready, 1)
            for t in range(KT):
                split_w_hi(0, t // 2, t % 2)
            for m in range(MT):
                for s in range(2):
                    act.wait_ge(xt_ready, 2 * m + s + 1)
                    act.activation(hT[:, m, KC * s:KC * (s + 1), :],
                                   tp[s][:, 0:KC * Q].rearrange("p (t q) -> p t q", q=Q), ACT.Relu)\
                       .then_inc(ht_ready, 1)
            act.wait_ge(ht_ready, 2 * MT)
            stage_hi(0, 0, 0)
            act.wait_ge(consts_ready, 5)
            act.wait_ge(keys_ready, 1)

            def phase(f):
                l, c, odd = phases[f]
                k = CH * l + c
                more = f + 1 < len(phases)

                def evacuate_h1t(n, m, s):
                    act.wait_ge(h1t_turned, n + 1)
                    turned = tp[s][:, 0:KC * Q]
                    if c == 0:
                        wait(act, spilled[s], 8 * (m - s))
                        act.activation(side[:, s, 0:KC * Q], turned, ACT.Copy).then_inc(h1t_ready, 1)
                    else:
                        act.activation(hT[:, m, KC:KT, :], turned.rearrange("p (t q) -> p t q", q=Q), ACT.Copy)\
                           .then_inc(h1t_ready, 1)

                def pair(i, last=False):
                    at_start = isinstance(i, int) and i == 0
                    for s in range(2):
                        m = 2 * i + s
                        u = MT * f + m
                        if f == 0:
                            source_hots(GPT * m, GPT * m, 0)
                        if not odd and not (at_start and s == 0):
                            act.wait_ge(tile_done, u)
                            evacuate_p(MT * k + m - 1, m - 1, 1 - s)
                        if f == 0:
                            source_hots(GPT * m + 1, GPT * m + 1, 1)
                        if not (last and s == 1):
                            stage_hi(u + 1, m + 1, 1 - s)
                            if odd:
                                stage_a(MT * k + m + 1, u + 1, m + 1, 1 - s)
                        elif more:
                            if (l, c, odd) == (0, CH - 1, 1):
                                act.wait_ge(reloaded, 16 * MT)
                                act.wait_ge(h1t_ready, MT * k + m - 1)
                            stage_hi(u + 1, 0, 0)
                        if f == 0:
                            source_hots(GPT * m + 2, GPT * m + 2, 0)
                        if more and not at_start:
                            split_w_hi(f + 1, i - 1, s)
                        if f == 0:
                            source_hots(GPT * m + 3, GPT * m + 3, 1)
                        if odd and l == 0 and not (at_start and s == 0):
                            evacuate_h1t(MT * c + m - 1, m - 1, 1 - s)

                if odd:
                    if f == 1:
                        act.wait_ge(a_ready, 1)
                    stage_a(MT * k, MT * f, 0, 0)
                pairs(act, pair, 0, MT // 2 - 1)
                pair(MT // 2 - 1, last=True)
                if not odd:
                    act.wait_ge(tile_done, MT * (f + 1))
                    evacuate_p(MT * k + MT - 1, MT - 1, 1)
                elif l == 0:
                    evacuate_h1t(MT * c + MT - 1, MT - 1, 1)
                    if c == CH - 1:
                        act.wait_ge(h1t_ready, MT * CH)

            phase(0)
            n_pass = act.value_load(passes_int[0:1, 0:1], min_val=1, max_val=N // WIN_D + 1)
            with act.If(n_pass > 1):
                with act.Fori(1, n_pass) as ps:
                    with act.Fori(0, NG // 2) as i:
                        for s in range(2):
                            source_hots(NG * ps + 2 * i + s, 2 * i + s, s)
            for f in range(1, len(phases)):
                phase(f)

        @block.vector
        def _(dve):
            steps = [0]

            def step(instruction):
                steps[0] += 1
                instruction.then_inc(vec_step, 1)
                dve.wait_ge(vec_step, steps[0])

            def destination_hots(n, g, s):
                wait(dve, win_ready, n - 1)
                for j in range(EJ):
                    hot = dve.tensor_scalar(dst_hot[:, s, j, :], iota_w[:], key_t[:, g, j:j + 1], None, ALU.is_equal)
                hot.then_inc(dst_hot_ready, 1)

            def add_window(n, g, s):
                start = dve.value_load(start_int[0:1, bass.ds(g, 1)], min_val=0, max_val=N * MT)
                dve.wait_ge(win_ready, n + 1)
                wait(dve, win_added, n)
                dve.tensor_tensor(AT[:, bass.ds(start, WIN)], win[s][:, 0:WIN], AT[:, bass.ds(start, WIN)],
                                  ALU.add).then_inc(win_added, 1)

            dve.wait_ge(edges_loaded, 32)
            dve.tensor_copy(dst_f[:], dst_i[:])
            step(dve.tensor_copy(src_f[:], src_i[:]))
            step(dve.tensor_scalar(negq[:], src_f[:], 1.0 / MT, -0.45, ALU.mult, ALU.add))
            dve.tensor_reduce(group_col[:, 0:1], dst_f[:], AX_X, ALU.min)
            step(dve.tensor_scalar(negq[:], negq[:], ROUND, None, ALU.add))
            dve.tensor_reduce(group_col[:, 1:2], dst_f[:], AX_X, ALU.max)
            step(dve.tensor_scalar(negq[:], negq[:], -ROUND, -1.0, ALU.add, ALU.mult))
            dve.tensor_scalar(group_col[:, 2:3], group_col[:, 0:1], float(MT), None, ALU.mult)
            step(dve.scalar_tensor_tensor(out=key[:], in0=negq[:], scalar=float(MT), in1=src_f[:],
                                          op0=ALU.mult, op1=ALU.add))
            dve.tensor_tensor(group_col[:, 3:4], group_col[:, 1:2], group_col[:, 0:1], ALU.subtract)
            step(dve.scalar_tensor_tensor(out=key[:], in0=dst_f[:], scalar=float(MT), in1=key[:],
                                          op0=ALU.mult, op1=ALU.add))
            dve.tensor_scalar(key[:], key[:], group_col[:, 2:3], None, ALU.subtract).then_inc(key_cols_ready, 1)
            for i in range(XP):
                dve.wait_ge(x_loaded[i], 16)
                for m in range(2 * i, 2 * i + 2):
                    for s in range(2):
                        last = dve.bn_stats(stats[:, m, s, :], x_all[:, m, CW * s:CW * (s + 1)])
            step(last)
            for m in range(MT):
                last = dve.bn_aggr(mean_var[:, m, :], stats[:, m])
            step(last)
            dve.tensor_scalar(rstd[:], mean_var[:, :, 1], EPS, None, ALU.add).then_inc(var_ready, 1)

            dve.wait_ge(keys_turned, 1)
            last = dve.tensor_copy(key_t[:], kp[0][0:EP, 0:EJ * NG].rearrange("p (j g) -> p g j", j=EJ))
            dve.tensor_copy(negq_t[:], kp[1][0:EP, 0:EJ * NG].rearrange("p (j g) -> p g j", j=EJ))
            rows = kp[0][0:1, EJ * NG:(EJ + 2) * NG]
            dve.tensor_copy(start_row[:], rows[:, 0:NG])
            dve.tensor_copy(start_int[:], rows[:, 0:NG])
            step(dve.tensor_reduce(row_f[:, 0:1], rows[:, NG:2 * NG], AX_X, ALU.max))
            step(dve.tensor_scalar(row_f[:, 1:2], row_f[:, 0:1], 1.0 / WIN_D, 0.5 / WIN_D - 0.5, ALU.mult, ALU.add))
            step(dve.tensor_scalar(row_f[:, 2:3], row_f[:, 1:2], ROUND, None, ALU.add))
            step(dve.tensor_scalar(passes_int[:], row_f[:, 2:3], -ROUND, 1.0, ALU.add, ALU.add))
            dve.sem_inc(keys_ready, 1)

            dve.wait_ge(std_ready, 1)
            step(dve.reciprocal(rstd[:], rstd[:]))
            for m in range(MT):
                dve.tensor_scalar(x_all[:, m, :], x_all[:, m, :], mean_var[:, m, 0:1], rstd[:, m:m + 1],
                                  ALU.subtract, ALU.mult).then_inc(xn_ready, 1)
            dve.wait_ge(consts_ready, 5)

            def evacuate_p(n, m, s):
                dve.wait_ge(p_hi_ready, n + 1)
                dve.tensor_tensor(p_lo[:, m, :], acc[s][:], p_hi[:, m, :].bitcast(F32),
                                  ALU.subtract).then_inc(p_lo_ready, 1)

            def edge_pair(i):
                at_start = isinstance(i, int) and i == 0
                for s in range(2):
                    m = 2 * i + s
                    for r in range(GPT):
                        g = GPT * m + r
                        destination_hots(g, g, r % 2)
                        if not (at_start and s == 0 and r == 0):
                            add_window(g - 1, g - 1, (r - 1) % 2)
                        if r == 0 and not (at_start and s == 0):
                            evacuate_p(m - 1, m - 1, 1 - s)

            pairs(dve, edge_pair)
            add_window(NG - 1, NG - 1, (NG - 1) % 2)
            evacuate_p(MT - 1, MT - 1, 1)
            n_pass = dve.value_load(passes_int[0:1, 0:1], min_val=1, max_val=N // WIN_D + 1)
            with dve.If(n_pass > 1):
                with dve.Fori(1, n_pass) as ps:
                    dve.wait_ge(dst_hot_ready, NG * ps)
                    dve.tensor_scalar(key_t[:], key_t[:], -float(WIN), None, ALU.add).then_inc(pass_keys, 1)
                    dve.tensor_scalar(start_row[:], start_row[:], float(WIN), float(N * MT), ALU.add, ALU.min)\
                       .then_inc(pass_keys, 1)
                    dve.wait_ge(pass_keys, 3 * ps - 1)
                    dve.tensor_copy(start_int[:], start_row[:]).then_inc(pass_keys, 1)
                    with dve.Fori(0, NG // 2) as i:
                        dve.wait_ge(pass_keys, 3 * ps)
                        for s in range(2):
                            destination_hots(NG * ps + 2 * i + s, 2 * i + s, s)
                            add_window(NG * ps + 2 * i + s, 2 * i + s, s)
            dve.wait_ge(win_added, NG * n_pass)
            dve.sem_inc(a_ready, 1)

            dve.wait_ge(bias_loaded, 16)
            for f in range(1, len(phases)):
                l, c, odd = phases[f]
                k = CH * l + c
                more = f + 1 < len(phases)

                def pair(i, last=False):
                    at_start = isinstance(i, int) and i == 0
                    for s in range(2):
                        m = 2 * i + s
                        u = MT * f + m
                        if not (last and s == 1):
                            stage_lo(dve, u + 1, m + 1, 1 - s)
                        elif more:
                            stage_lo(dve, u + 1, 0, 0)
                        if more and not at_start:
                            split_w_lo(dve, f + 1, i - 1, s)
                        if not odd:
                            evacuate_p(MT * k + m, m, s)
                            continue
                        n = MT * k + m
                        if l == 0:
                            wait(dve, h1t_turned, n - 1)
                            addend = bias[:, c * CW:(c + 1) * CW]
                        else:
                            wait(dve, stored[s], 16 * (c * (MT // 2) + i))
                            dve.wait_ge(xres_ready, MT * c + m + 1)
                            addend = side[0:Q, s, :]
                        dve.wait_ge(tile_done, u + 1)
                        dve.tensor_tensor(tile_out[:, s, :], acc[s][:], addend, ALU.add).then_inc(out_ready, 1)

                pairs(dve, pair, 0, MT // 2 - 1)
                pair(MT // 2 - 1, last=True)

        @block.tensor
        def _(pe):
            def count_group(n, s):
                pe.wait_ge(src_hot_ready, n + 1)
                pe.wait_ge(dst_hot_ready, n + 1)
                wait(pe, win_added, n - 1)
                for j in range(EJ):
                    mm = pe.matmul(win[s][:, 0:WIN], src_hot[:, s, j, :], dst_hot[:, s, j, :],
                                   start=(j == 0), stop=(j == EJ - 1))
                mm.then_inc(win_ready, 1)

            def times_weights(f, s, t, start, stop):
                w = w_hi[f % 2][:, t, :], w_lo[f % 2][:, t, :]
                pe.matmul(acc[s][:], lhs_hi[:, s, t, :], w[0], start=start, stop=False)
                pe.matmul(acc[s][:], lhs_hi[:, s, t, :], w[1], start=False, stop=False)
                return pe.matmul(acc[s][:], lhs_lo[:, s, t, :], w[0], start=False, stop=stop)

            pe.wait_ge(consts_ready, 2)
            pe.wait_ge(key_cols_ready, 1)
            for j in range(EJ):
                of_tile = slice(j * NG, (j + 1) * NG)
                for what, to in ((key, kp[0]), (negq, kp[1])):
                    pe.transpose(to[0:EP, of_tile], what[:].rearrange("g (p j) -> g j p", j=EJ)[:, j], ident[0:NG, 0:NG])
            for r in range(2):
                row = pe.transpose(kp[0][0:1, (EJ + r) * NG:(EJ + r + 1) * NG], group_col[:, 2 + r:3 + r],
                                   ident[0:NG, 0:NG])
            row.then_inc(keys_turned, 1)
            for m in range(MT):
                pe.wait_ge(xn_ready, m + 1)
                for s in range(2):
                    wait(pe, ht_ready, 2 * m + s - 1)
                    for t in range(KC):
                        col = (KC * s + t) * P
                        turned = pe.transpose(tp[s][:, t * Q:(t + 1) * Q], x_all[:, m, col:col + P], ident[0:Q, 0:Q])
                    turned.then_inc(xt_ready, 1)

            for f, (l, c, odd) in enumerate(phases):
                k = CH * l + c

                def pair(i):
                    at_start = isinstance(i, int) and i == 0
                    for s in range(2):
                        m = 2 * i + s
                        u = MT * f + m
                        if f == 0:
                            count_group(GPT * m, 0)
                        if at_start and s == 0:
                            pe.wait_ge(w_hi_ready, KT * (f + 1))
                            pe.wait_ge(w_lo_ready, KT * (f + 1))
                            if odd:
                                pe.wait_ge(p_lo_ready, MT * (k + 1))
                        if at_start and not odd:
                            wait(pe, out_ready, MT * k - 1 + s)
                        if not at_start:
                            pe.wait_ge(out_ready if odd else p_lo_ready, MT * k + m - 1)
                        if odd:
                            pe.wait_ge(a_hi_ready, MT * k + m + 1)
                            for j in range(MT):
                                for part in (p_hi, p_lo):
                                    pe.matmul(acc[s][:], a_hi[:, s, j, :], part[:, j, :],
                                              start=(j == 0 and part is p_hi), stop=False)
                        pe.wait_ge(lhs_hi_ready, u + 1)
                        pe.wait_ge(lhs_lo_ready, u + 1)
                        for t in range(KT):
                            if f == 0 and t % 2 == 0 and t > 0:
                                count_group(GPT * m + t // 2, (t // 2) % 2)
                            mm = times_weights(f, s, t, start=(t == 0 and not odd), stop=(t == KT - 1))
                        mm.then_inc(tile_done, 1)
                        if l == 0 and odd and not (at_start and s == 0):
                            turn_h1(MT * c + m - 1, 1 - s)

                def turn_h1(n, s):
                    pe.wait_ge(out_ready, n + 1)
                    wait(pe, h1t_ready, n - 1)
                    for t in range(KC):
                        turned = pe.transpose(tp[s][:, t * Q:(t + 1) * Q], tile_out[:, s, t * P:(t + 1) * P],
                                              ident[0:Q, 0:Q])
                    turned.then_inc(h1t_turned, 1)

                pairs(pe, pair)
                if l == 0 and odd:
                    turn_h1(MT * c + MT - 1, 1)
                if f == 0:
                    n_pass = pe.value_load(passes_int[0:1, 0:1], min_val=1, max_val=N // WIN_D + 1)
                    with pe.If(n_pass > 1):
                        with pe.Fori(1, n_pass) as ps:
                            with pe.Fori(0, NG // 2) as i:
                                for s in range(2):
                                    count_group(NG * ps + 2 * i + s, s)


_INS = ["x", "src", "dst", "L0_gnn_Ws1", "L0_gnn_Wn1", "L0_gnn_b1", "L0_gnn_Ws2", "L0_gnn_Wn2", "L0_gnn_b2"]


def kernel(**inputs):
    import numpy as _np
    import concourse.bacc as _bacc
    from concourse import mybir as _mybir
    from concourse.bass_utils import run_bass_kernel_spmd as _run

    nc = _bacc.Bacc("TRN2", target_bir_lowering=False, num_devices=1, dynamic_dma_scratch_size=1024)
    arrays, aps = {}, {}
    for name in _INS:
        a = _np.ascontiguousarray(inputs[name])
        arrays[f"in_{name}"] = a
        aps[name] = nc.dram_tensor(f"in_{name}", a.shape, _mybir.dt.from_np(a.dtype), kind="ExternalInput").ap()
    shape = arrays["in_x"].shape
    out = nc.dram_tensor("out_h", shape, _mybir.dt.float32, kind="ExternalOutput").ap()
    gnn_program(nc, aps["x"], aps["src"], aps["dst"], [aps["L0_gnn_Ws1"], aps["L0_gnn_Ws2"]],
                [aps["L0_gnn_Wn1"], aps["L0_gnn_Wn2"]], [aps["L0_gnn_b1"], aps["L0_gnn_b2"]], out)
    r = _run(nc, [arrays], core_ids=[0])
    return r.results[0]["out_h"]
```

```python
from contextlib import ExitStack

import concourse.bass as bass
from concourse import mybir

ALU = mybir.AluOpType
ACT = mybir.ActivationFunctionType
AX_X = mybir.AxisListType.X
F32 = mybir.dt.float32
F32R = mybir.dt.float32r
F16 = mybir.dt.float16
BF16 = mybir.dt.bfloat16
I32 = mybir.dt.int32
U32 = mybir.dt.uint32
U16 = mybir.dt.uint16

P = 128
EPS = 1e-5
ROUND = float(3 * 2 ** 22)


def gnn_program(nc, x, src, dst, Ws, Wn, b, out):
    N, D = x.shape
    E = src.shape[0]
    MT = 10
    Q = N // MT
    KT = D // P
    CH = 2
    CW = D // CH
    KC = CW // P
    EP = 125
    EJ = 8
    GE = EP * EJ
    NG = E // GE
    WIN_D = 40
    WIN = WIN_D * MT
    FIRST, GPT = 4, 2
    BPT, BT = 2, MT - 2
    LATE = NG - BPT * BT
    HJ = EJ // 2
    BY_ACT = 3, 2
    EXACT = 4096
    COL_START, COL_END, COL_ONE = 2, 3, 4
    N_PASS, SLOW, MANY = 0, 1, 2
    assert N == MT * Q and NG * GE == E and WIN <= 512 and Q <= P and MT % 2 == 0
    assert 2 * FIRST + GPT * (MT - 2) == LATE and FIRST % 2 == GPT % 2 == BPT % 2 == 0

    def early_groups(i, s):
        if isinstance(i, int) and i == 0:
            return [FIRST * s + r for r in range(FIRST)]
        return [2 * FIRST + GPT * (2 * i + s - 2) + r for r in range(GPT)]

    x_rows = x.rearrange("(q m) d -> q (m d)", m=MT)
    x_tiles = x.rearrange("(m r) d -> m r d", m=MT)
    out_tiles = out.rearrange("(m r) d -> m r d", m=MT)
    w_tiles = [[W.rearrange("(t p) n -> p t n", p=P) for W in pair] for pair in zip(Wn, Ws)]
    h1_spill = nc.dram_tensor("h1_spill", [MT, P, KC * Q], F32).ap()

    phases = [(l, c, odd) for l in range(2) for c in range(CH) for odd in range(2)]
    XP = MT // 2
    LN_AT = {0: (0, 6), 6: (6, MT)}

    with ExitStack() as ctx:
        def sb(name, shape, dt):
            return ctx.enter_context(nc.sbuf_tensor(name, shape, dt))

        def psum(name, shape, dt=F32):
            return ctx.enter_context(nc.psum_tensor(name, shape, dt))

        def sem(name):
            return ctx.enter_context(nc.semaphore(name))

        hT = sb("hT", [P, KT, N], F32)
        lhs_hi = sb("lhs_hi", [P, 2, KT, Q], F32R)
        lhs_lo = sb("lhs_lo", [P, 2, KT, Q], F32R)
        AT = sb("AT", [Q, N * MT + WIN], U16)
        w_raw = sb("w_raw", [P, 2, CW], F32)
        wn_hi = sb("wn_hi", [P, KT, CW], F32R)
        wn_lo = sb("wn_lo", [P, KT, CW], F32R)
        bias = sb("bias", [Q, CW], F32)
        ident = sb("ident", [P, P], F32)
        iota_w = sb("iota_w", [EP, WIN], F16)
        iota_q = sb("iota_q", [EP, Q], F16)
        iota_negq = sb("iota_negq", [EP, Q], F16)
        key_t = sb("key_t", [EP, NG, EJ], F32)
        negq_t = sb("negq_t", [EP, NG, EJ], F32)
        stats = sb("stats", [Q, MT, 2, 6], F32)
        mean_var = sb("mean_var", [Q, MT, 2], F32)
        rstd = sb("rstd", [Q, MT], F32)
        group_col = sb("group_col", [NG, 8], F32)
        start_row = sb("start_row", [1, NG], F32)
        start_int = sb("start_int", [1, NG], I32)
        rows = sb("rows", [1, 2, NG], F32)
        order_row = sb("order_row", [1, 2, NG], F32)
        row_f = sb("row_f", [1, 8], F32)
        ones_row = sb("ones_row", [1, NG], F32)
        overlap = sb("overlap", [NG, 2, NG], F32)
        flags = sb("flags", [1, 3], I32)

        with ExitStack() as early:
            def early_sb(name, shape, dt):
                return early.enter_context(nc.sbuf_tensor(name, shape, dt))

            x_all = early_sb("x_all", [Q, MT, D], F32)
            dst_i = early_sb("dst_i", [NG, GE], I32)
            src_i = early_sb("src_i", [NG, GE], I32)
            dst_f = early_sb("dst_f", [NG, GE], F32)
            src_f = early_sb("src_f", [NG, GE], F32)
            negq = early_sb("negq", [NG, GE], F32)
            key = early_sb("key", [NG, GE], F32)
        p_hi = sb("p_hi", [Q, MT, CW], F32R)
        p_lo = sb("p_lo", [Q, MT, CW], F32R)
        ws_hi = sb("ws_hi", [P, KT, CW], F32R)
        ws_lo = sb("ws_lo", [P, KT, CW], F32R)
        dst_hot = sb("dst_hot", [EP, 2, HJ, WIN], BF16)
        src_hot = sb("src_hot", [EP, 2, HJ, Q], BF16)
        a_hi = sb("a_hi", [Q, 2, MT, Q], F32R)
        tile_out = sb("tile_out", [Q, 2, CW], F32)
        side = sb("side", [P, 2, CW], F32)

        w_hi, w_lo = [wn_hi, ws_hi], [wn_lo, ws_lo]

        def node_tile(odd, m, t0=0, t1=KT):
            if odd:
                return hT[:, t0:t1, :].rearrange("p t (m r) -> p m t r", m=MT)[:, m]
            return hT[:, t0:t1, :].rearrange("p t (q m) -> p m t q", m=MT)[:, m]

        def at_block(m):
            return AT[:, 0:N * MT].rearrange("p (m r c) -> p m c r", m=MT, c=MT)[:, m]

        acc = [psum(f"acc{s}", [Q, CW]) for s in range(2)]
        win = [psum(f"win{s}", [Q, 512]) for s in range(2)]
        tp = [psum(f"tp{s}", [P, 512]) for s in range(2)]
        kp = [psum(f"kp{s}", [P, 512]) for s in range(2)]

        edges_loaded = sem("edges_loaded")
        x_loaded = [sem(f"x_loaded{i}") for i in range(XP)]
        bias_loaded = sem("bias_loaded")
        w_raw_loaded = [sem(f"w_raw_loaded{s}") for s in range(2)]
        w_hi_ready = sem("w_hi_ready")
        w_lo_ready = sem("w_lo_ready")
        consts_ready = sem("consts_ready")
        at_zeroed = sem("at_zeroed")
        vec_step = sem("vec_step")
        key_cols_ready = sem("key_cols_ready")
        keys_turned = sem("keys_turned")
        rows_ready = sem("rows_ready")
        rows_spread = sem("rows_spread")
        overlap_ready = sem("overlap_ready")
        overlap_summed = sem("overlap_summed")
        flags_ready = sem("flags_ready")
        keys_ready = sem("keys_ready")
        var_ready = sem("var_ready")
        std_ready = sem("std_ready")
        xn_ready = sem("xn_ready")
        xt_ready = sem("xt_ready")
        ht_ready = sem("ht_ready")
        src_sq_ready = sem("src_sq_ready")
        src_hot_ready = sem("src_hot_ready")
        dst_hot_ready = sem("dst_hot_ready")
        hots_used = sem("hots_used")
        win_added = sem("win_added")
        pass_keys = sem("pass_keys")
        a_ready = sem("a_ready")
        lhs_hi_ready = sem("lhs_hi_ready")
        lhs_lo_ready = sem("lhs_lo_ready")
        tile_done = sem("tile_done")
        p_hi_ready = sem("p_hi_ready")
        p_lo_ready = sem("p_lo_ready")
        a_hi_ready = sem("a_hi_ready")
        a_hi_used = sem("a_hi_used")
        a_lo_ready = sem("a_lo_ready")
        out_ready = sem("out_ready")
        h1t_turned = sem("h1t_turned")
        h1t_ready = sem("h1t_ready")
        spilled = [sem(f"spilled{s}") for s in range(2)]
        reloaded = sem("reloaded")
        xres_loaded = [sem(f"xres_loaded{s}") for s in range(2)]
        xres_ready = sem("xres_ready")
        stored = [sem(f"stored{s}") for s in range(2)]

        def wait(eng, s, count):
            if not isinstance(count, int) or count > 0:
                eng.wait_ge(s, count)

        def pairs(eng, body, first=0, last=MT // 2):
            body(first)
            with eng.Fori(first + 1, last) as i:
                body(i)

        block = ctx.enter_context(nc.Block())

        @block.sync
        def _(sp):
            def load_w(f, t, s):
                l, c, odd = phases[f]
                wait(sp, w_hi_ready, KT * f + t - 1)
                wait(sp, w_lo_ready, KT * f + t - 1)
                sp.dma_start(w_raw[:, s, :], w_tiles[l][odd][:, t, c * CW:(c + 1) * CW]).then_inc(w_raw_loaded[s], 16)

            sp.dma_start(dst_i[:], dst.rearrange("(g e) -> g e", g=NG)).then_inc(edges_loaded, 16)
            sp.dma_start(src_i[:], src.rearrange("(g e) -> g e", g=NG)).then_inc(edges_loaded, 16)
            for i in range(XP):
                if i < KT // 2:
                    load_w(0, 2 * i, 0)
                    load_w(0, 2 * i + 1, 1)
                sp.dma_start(x_all[:, 2 * i:2 * i + 2, :], x_rows[:, 2 * i * D:(2 * i + 2) * D]).then_inc(x_loaded[i], 16)
            sp.dma_start(bias[:], b[0][0:CW].partition_broadcast(Q)).then_inc(bias_loaded, 16)

            for f, (l, c, odd) in enumerate(phases):
                chunk = slice(c * CW, (c + 1) * CW)
                k = CH * l + c
                if k > 0 and odd == 0:
                    sp.wait_ge(out_ready, MT * k)
                    sp.dma_start(bias[:], b[l][chunk].partition_broadcast(Q)).then_inc(bias_loaded, 16)
                if l == 1 and odd == 1:
                    for s in range(2):
                        wait(sp, out_ready, MT * k)
                        sp.dma_start(side[0:Q, s, :], x_tiles[s][:, chunk]).then_inc(xres_loaded[s], 16)

                def pair(i, last=False):
                    if f + 1 < len(phases) and not last:
                        for s in range(2):
                            load_w(f + 1, 2 * i + s, s)
                    if not odd:
                        return
                    for s in range(2):
                        m = 2 * i + s
                        if l == 0 and c == 0:
                            sp.wait_ge(h1t_ready, m + 1)
                            sp.dma_start(h1_spill[m], side[:, s, 0:KC * Q]).then_inc(spilled[s], 16)
                        if l == 0 and c == 1:
                            sp.wait_ge(lhs_hi_ready, MT * f + m + 1)
                            sp.wait_ge(lhs_lo_ready, MT * f + m + 1)
                            sp.dma_start(node_tile(1, m, 0, KC), h1_spill[m].rearrange("p (t q) -> p t q", q=Q))\
                              .then_inc(reloaded, 16)
                        if l == 1:
                            sp.wait_ge(out_ready, MT * k + m + 1)
                            sp.dma_start(out_tiles[m][:, chunk], tile_out[:, s, :]).then_inc(stored[s], 16)
                            if not last:
                                sp.dma_start(side[0:Q, s, :], x_tiles[m + 2][:, chunk]).then_inc(xres_loaded[s], 16)

                if l == 0 and c == 1 and odd == 1:
                    for s in range(2):
                        sp.wait_ge(spilled[s], 16 * (MT // 2))
                if odd or f + 1 < len(phases):
                    pairs(sp, pair, 0, MT // 2 - 1)
                    pair(MT // 2 - 1, last=True)
            for s in range(2):
                sp.wait_ge(stored[s], 16 * CH * (MT // 2))

        def split_w_lo(eng, f, n, s):
            t = 2 * n + s
            eng.wait_ge(w_hi_ready, KT * f + t + 1)
            eng.tensor_tensor(w_lo[f % 2][:, t, :], w_raw[:, s, :], w_hi[f % 2][:, t, :].bitcast(F32),
                              ALU.subtract).then_inc(w_lo_ready, 1)

        def stage_lo(eng, u, odd, m, s):
            eng.wait_ge(lhs_hi_ready, u + 1)
            eng.tensor_tensor(lhs_lo[:, s], node_tile(odd, m), lhs_hi[:, s].bitcast(F32),
                              ALU.subtract).then_inc(lhs_lo_ready, 1)

        @block.gpsimd
        def _(pool):
            pool.memset(ident[:], 0.0).then_inc(consts_ready, 1)
            pool.memset(ones_row[:], 1.0).then_inc(consts_ready, 1)
            pool.wait_ge(consts_ready, 2)
            pool.affine_select(out=ident[:], in_=ident[:], compare_op=ALU.not_equal, fill=1.0, base=0,
                               pattern=[[-1, P]], channel_multiplier=1).then_inc(consts_ready, 1)
            pool.iota(iota_q[:], [[1, Q]], base=0, channel_multiplier=0,
                      allow_small_or_imprecise_dtypes=True).then_inc(consts_ready, 1)
            pool.iota(iota_negq[:], [[-1, Q]], base=0, channel_multiplier=0,
                      allow_small_or_imprecise_dtypes=True).then_inc(consts_ready, 1)
            pool.iota(iota_w[:], [[1, WIN]], base=0, channel_multiplier=0,
                      allow_small_or_imprecise_dtypes=True).then_inc(consts_ready, 1)
            pool.iota(order_row[:, 0, :].rearrange("o (j r) -> o j r", r=BPT), [[Q * MT, NG // BPT], [0, BPT]],
                      base=(1 - (LATE - BPT) // BPT) * Q * MT, channel_multiplier=0,
                      allow_small_or_imprecise_dtypes=True).then_inc(consts_ready, 1)
            for t in range(KT):
                split_w_lo(pool, 0, t // 2, t % 2)
            pool.memset(AT[:].bitcast(U32), 0).then_inc(at_zeroed, 1)
            stage_lo(pool, 0, 0, 0, 0)

            def pair(i, last=False):
                for s in range(2):
                    m = 2 * i + s
                    if last and s == 1:
                        stage_lo(pool, MT, 1, 0, 0)
                    else:
                        stage_lo(pool, m + 1, 0, m + 1, 1 - s)
                    if not (isinstance(i, int) and i == 0):
                        split_w_lo(pool, 1, i - 1, s)

            pairs(pool, pair, 0, MT // 2 - 1)
            pair(MT // 2 - 1, last=True)

            for c in range(CH):
                pool.wait_ge(bias_loaded, 16 * (CH + c + 1))

                def add_bias(i):
                    for s in range(2):
                        pool.wait_ge(xres_loaded[s], 16 * (c * (MT // 2) + i + 1))
                        pool.tensor_tensor(side[0:Q, s, :], side[0:Q, s, :], bias[:], ALU.add).then_inc(xres_ready, 1)

                pairs(pool, add_bias)

        @block.scalar
        def _(act):
            def split_w_hi(f, n, s):
                act.wait_ge(w_raw_loaded[s], 16 * (KT // 2 * f + n + 1))
                act.activation(w_hi[f % 2][:, 2 * n + s, :], w_raw[:, s, :], ACT.Copy).then_inc(w_hi_ready, 1)

            def stage_hi(u, odd, m, s):
                wait(act, tile_done, u - 1)
                act.activation(lhs_hi[:, s], node_tile(odd, m), ACT.Copy).then_inc(lhs_hi_ready, 1)

            def stage_a(n, u, m, s):
                wait(act, tile_done, u - 1)
                act.activation(a_hi[:, s], at_block(m), ACT.Copy).then_inc(a_hi_ready, 1)

            def evacuate_p(n, m, s):
                act.activation(p_hi[:, m, :], acc[s][:], ACT.Copy).then_inc(p_hi_ready, 1)

            def source_hots(n, g):
                for h in range(2):
                    wait(act, hots_used, 2 * n + h - 1)
                    for j in range(BY_ACT[h]):
                        at = HJ * h + j
                        square = act.activation(src_hot[:, h, j, :], iota_q[:], ACT.Square, bias=negq_t[:, g, at:at + 1])
                    square.then_inc(src_sq_ready, 1)
                    act.wait_ge(src_sq_ready, 2 * n + h + 1)
                    share = src_hot[:, h, 0:BY_ACT[h], :]
                    act.activation(share, share, ACT.Relu, bias=1.0, scale=-1.0).then_inc(src_hot_ready, 1)

            for t in range(KT):
                split_w_hi(0, t // 2, t % 2)
            for m in range(MT):
                if m in LN_AT:
                    part = slice(*LN_AT[m])
                    act.wait_ge(var_ready, list(LN_AT).index(m) + 1)
                    act.activation(rstd[:, part], rstd[:, part], ACT.Sqrt).then_inc(std_ready, 1)
                for s in range(2):
                    act.wait_ge(xt_ready, 2 * m + s + 1)
                    act.activation(node_tile(0, m, KC * s, KC * (s + 1)),
                                   tp[s][:, 0:KC * Q].rearrange("p (t q) -> p t q", q=Q), ACT.Relu)\
                       .then_inc(ht_ready, 1)
            act.wait_ge(ht_ready, 2 * MT)
            stage_hi(0, 0, 0, 0)
            act.wait_ge(consts_ready, 7)
            act.wait_ge(keys_ready, 2)

            def phase(f, beside=False):
                l, c, odd = phases[f]
                k = CH * l + c
                more = f + 1 < len(phases)

                def evacuate_h1t(n, m, s):
                    act.wait_ge(h1t_turned, n + 1)
                    turned = tp[s][:, 0:KC * Q]
                    if c == 0:
                        wait(act, spilled[s], 8 * (m - s))
                        act.activation(side[:, s, 0:KC * Q], turned, ACT.Copy).then_inc(h1t_ready, 1)
                    else:
                        act.activation(node_tile(1, m, KC, KT), turned.rearrange("p (t q) -> p t q", q=Q), ACT.Copy)\
                           .then_inc(h1t_ready, 1)

                new_h = (l, c, odd) == (0, CH - 1, 1)

                def pair(i, last=False):
                    at_start = isinstance(i, int) and i == 0
                    for s in range(2):
                        m = 2 * i + s
                        u = MT * f + m
                        groups = early_groups(i, s) if f == 0 else []
                        for g in groups[:1]:
                            source_hots(g, g)
                        if not odd and not (at_start and s == 0):
                            act.wait_ge(tile_done, u)
                            evacuate_p(MT * k + m - 1, m - 1, 1 - s)
                        if not (last and s == 1):
                            stage_hi(u + 1, odd, m + 1, 1 - s)
                            if odd:
                                if beside:
                                    act.wait_ge(win_added, LATE - BPT + BPT * (m + 1))
                                stage_a(MT * k + m + 1, u + 1, m + 1, 1 - s)
                        elif more and not new_h:
                            stage_hi(u + 1, 1 - odd, 0, 0)
                        for g in groups[1:]:
                            source_hots(g, g)
                        if more and not at_start:
                            split_w_hi(f + 1, i - 1, s)
                        if beside and not last:
                            for g in range(BPT):
                                source_hots(LATE + BPT * m + g, LATE + BPT * m + g)
                        if odd and l == 0 and not (at_start and s == 0):
                            evacuate_h1t(MT * c + m - 1, m - 1, 1 - s)

                if odd:
                    if beside:
                        act.wait_ge(win_added, LATE - BPT)
                    elif c == 0 or f == CH * 2 - 1:
                        act.wait_ge(a_ready, 1)
                    stage_a(MT * k, MT * f, 0, 0)
                pairs(act, pair, 0, MT // 2 - 1)
                pair(MT // 2 - 1, last=True)
                if not odd:
                    act.wait_ge(tile_done, MT * (f + 1))
                    evacuate_p(MT * k + MT - 1, MT - 1, 1)
                elif l == 0:
                    evacuate_h1t(MT * c + MT - 1, MT - 1, 1)
                    if new_h:
                        act.wait_ge(h1t_ready, MT * CH)
                        act.wait_ge(reloaded, 16 * MT)
                        stage_hi(MT * (f + 1), 0, 0, 0)

            phase(0)
            act.wait_ge(flags_ready, 1)
            n_pass = act.value_load(flags[0:1, N_PASS:N_PASS + 1], min_val=1, max_val=N // WIN_D + 1)
            slow = act.value_load(flags[0:1, SLOW:SLOW + 1], min_val=0, max_val=1)
            with act.If(slow > 0):
                with act.Fori(LATE // 2, NG // 2) as i:
                    for s in range(2):
                        source_hots(2 * i + s, 2 * i + s)
                with act.If(n_pass > 1):
                    with act.Fori(1, n_pass) as ps:
                        with act.Fori(0, NG // 2) as i:
                            for s in range(2):
                                source_hots(NG * ps + 2 * i + s, 2 * i + s)
                phase(1)
            with act.Else():
                phase(1, beside=True)
            for f in range(2, len(phases)):
                phase(f)

        @block.vector
        def _(dve):
            steps = [0]

            def step(instruction):
                steps[0] += 1
                instruction.then_inc(vec_step, 1)
                dve.wait_ge(vec_step, steps[0])

            def destination_hots(n, g):
                for h in range(2):
                    wait(dve, hots_used, 2 * n + h - 1)
                    for j in range(HJ):
                        at = HJ * h + j
                        if j >= BY_ACT[h]:
                            dve.tensor_scalar(src_hot[:, h, j, :], iota_negq[:], negq_t[:, g, at:at + 1], None,
                                              ALU.is_equal)
                        hot = dve.tensor_scalar(dst_hot[:, h, j, :], iota_w[:], key_t[:, g, at:at + 1], None,
                                                ALU.is_equal)
                    hot.then_inc(dst_hot_ready, 1)

            def add_window(n, g, s):
                start = dve.value_load(start_int[0:1, bass.ds(g, 1)], min_val=0, max_val=N * MT)
                dve.wait_ge(hots_used, 2 * n + 2)
                wait(dve, win_added, n)
                dve.tensor_tensor(AT[:, bass.ds(start, WIN)], win[s][:, 0:WIN], AT[:, bass.ds(start, WIN)],
                                  ALU.add).then_inc(win_added, 1)

            dve.wait_ge(edges_loaded, 32)
            dve.tensor_copy(dst_f[:], dst_i[:])
            step(dve.tensor_copy(src_f[:], src_i[:]))
            step(dve.tensor_scalar(negq[:], src_f[:], 1.0 / MT, -0.45, ALU.mult, ALU.add))
            dve.tensor_reduce(group_col[:, 0:1], dst_f[:], AX_X, ALU.min)
            step(dve.tensor_scalar(negq[:], negq[:], ROUND, None, ALU.add))
            dve.tensor_reduce(group_col[:, 1:2], dst_f[:], AX_X, ALU.max)
            step(dve.tensor_scalar(negq[:], negq[:], -ROUND, -1.0, ALU.add, ALU.mult))
            dve.tensor_scalar(group_col[:, COL_START:COL_START + 1], group_col[:, 0:1], float(MT), None, ALU.mult)
            dve.tensor_scalar(group_col[:, COL_END:COL_END + 1], group_col[:, 1:2], float(MT), None, ALU.mult)
            dve.memset(group_col[:, COL_ONE:COL_ONE + 1], 1.0)
            step(dve.scalar_tensor_tensor(out=key[:], in0=negq[:], scalar=float(MT), in1=src_f[:],
                                          op0=ALU.mult, op1=ALU.add))
            step(dve.scalar_tensor_tensor(out=key[:], in0=dst_f[:], scalar=float(MT), in1=key[:],
                                          op0=ALU.mult, op1=ALU.add))
            dve.tensor_scalar(key[:], key[:], group_col[:, COL_START:COL_START + 1], None,
                              ALU.subtract).then_inc(key_cols_ready, 1)
            dve.wait_ge(keys_turned, 1)
            dve.tensor_copy(key_t[:], kp[0][0:EP, 0:EJ * NG].rearrange("p (j g) -> p g j", j=EJ)).then_inc(keys_ready, 1)
            turned = kp[1][0:EP, 0:EJ * NG].rearrange("p (j g) -> p g j", j=EJ)
            dve.tensor_copy(negq_t[:], turned).then_inc(keys_ready, 1)
            first_row, second_row = (kp[r][0:1, EJ * NG:(EJ + 1) * NG] for r in range(2))
            dve.tensor_copy(start_row[:], first_row)
            dve.tensor_copy(start_int[:], first_row)
            dve.tensor_copy(rows[:, 0, :], first_row)
            dve.tensor_copy(rows[:, 1, :], second_row).then_inc(rows_ready, 1)
            for n, (first, last) in enumerate(LN_AT.values()):
                for m in range(first, last):
                    if m % 2 == 0:
                        dve.wait_ge(x_loaded[m // 2], 16)
                    for s in range(2):
                        stat = dve.bn_stats(stats[:, m, s, :], x_all[:, m, CW * s:CW * (s + 1)])
                step(stat)
                for m in range(first, last):
                    stat = dve.bn_aggr(mean_var[:, m, :], stats[:, m])
                step(stat)
                dve.tensor_scalar(rstd[:, first:last], mean_var[:, first:last, 1], EPS, None, ALU.add)\
                   .then_inc(var_ready, 1)
                dve.wait_ge(std_ready, n + 1)
                step(dve.reciprocal(rstd[:, first:last], rstd[:, first:last]))
                for m in range(first, last):
                    dve.tensor_scalar(x_all[:, m, :], x_all[:, m, :], mean_var[:, m, 0:1], rstd[:, m:m + 1],
                                      ALU.subtract, ALU.mult).then_inc(xn_ready, 1)
            dve.wait_ge(consts_ready, 7)
            dve.wait_ge(keys_ready, 2)
            def set_flags():
                dve.wait_ge(rows_ready, 1)
                step(dve.tensor_tensor(order_row[:, 1, :], rows[:, 1, :], rows[:, 0, :], ALU.subtract))
                step(dve.tensor_reduce(row_f[:, 0:1], order_row[:, 1, :], AX_X, ALU.max))
                step(dve.tensor_scalar(row_f[:, 0:1], row_f[:, 0:1], 1.0 / WIN, 0.5 / WIN_D - 0.5, ALU.mult, ALU.add))
                step(dve.tensor_scalar(row_f[:, 0:1], row_f[:, 0:1], ROUND, None, ALU.add))
                step(dve.tensor_scalar(row_f[:, 0:1], row_f[:, 0:1], -ROUND, 1.0, ALU.add, ALU.add))
                dve.tensor_copy(flags[:, N_PASS:N_PASS + 1], row_f[:, 0:1])
                step(dve.tensor_tensor(order_row[:, 1, :], rows[:, 0, :], order_row[:, 0, :], ALU.is_ge))
                step(dve.tensor_reduce(row_f[:, 1:2], order_row[:, 1, :], AX_X, ALU.min))
                step(dve.tensor_scalar(row_f[:, 2:3], row_f[:, 0:1], 1.5, row_f[:, 1:2], ALU.is_lt, ALU.mult))
                step(dve.tensor_scalar(flags[:, SLOW:SLOW + 1], row_f[:, 2:3], -1.0, 1.0, ALU.mult, ALU.add))
                dve.wait_ge(rows_spread, 1)
                spread = kp[1][0:NG, 0:2 * NG]
                step(dve.tensor_scalar(overlap[:, 0, :], spread[:, 0:NG], group_col[:, COL_END:COL_END + 1], None,
                                       ALU.is_le))
                dve.scalar_tensor_tensor(out=overlap[:, 1, :], in0=spread[:, NG:2 * NG],
                                         scalar=group_col[:, COL_START:COL_START + 1], in1=overlap[:, 0, :],
                                         op0=ALU.is_ge, op1=ALU.mult).then_inc(overlap_ready, 1)
                dve.wait_ge(overlap_summed, 1)
                step(dve.tensor_reduce(row_f[:, 3:4], kp[0][0:1, 0:NG], AX_X, ALU.max))
                dve.tensor_scalar(flags[:, MANY:MANY + 1], row_f[:, 3:4], float(EXACT // GE), None,
                                  ALU.is_gt).then_inc(flags_ready, 1)

            def evacuate_p(n, m, s):
                dve.wait_ge(p_hi_ready, n + 1)
                dve.tensor_tensor(p_lo[:, m, :], acc[s][:], p_hi[:, m, :].bitcast(F32),
                                  ALU.subtract).then_inc(p_lo_ready, 1)

            def edge_pair(i):
                at_start = isinstance(i, int) and i == 0
                for s in range(2):
                    m = 2 * i + s
                    for r, g in enumerate(early_groups(i, s)):
                        destination_hots(g, g)
                        if not (at_start and s == 0 and r == 0):
                            add_window(g - 1, g - 1, (r + 1) % 2)
                        if r == 0 and not (at_start and s == 0):
                            evacuate_p(m - 1, m - 1, 1 - s)
                    if at_start and s == 0:
                        set_flags()

            dve.wait_ge(at_zeroed, 1)
            pairs(dve, edge_pair)
            add_window(LATE - 1, LATE - 1, (LATE - 1) % 2)
            evacuate_p(MT - 1, MT - 1, 1)

            dve.wait_ge(lhs_lo_ready, MT + 1)
            dve.wait_ge(w_lo_ready, 2 * KT)
            dve.wait_ge(bias_loaded, 16)
            n_pass = dve.value_load(flags[0:1, N_PASS:N_PASS + 1], min_val=1, max_val=N // WIN_D + 1)
            slow = dve.value_load(flags[0:1, SLOW:SLOW + 1], min_val=0, max_val=1)
            many = dve.value_load(flags[0:1, MANY:MANY + 1], min_val=0, max_val=1)

            def phase(f, beside=False):
                l, c, odd = phases[f]
                k = CH * l + c
                more = f + 1 < len(phases)
                new_h = (l, c, odd) == (0, CH - 1, 1)

                def pair(i, last=False):
                    at_start = isinstance(i, int) and i == 0
                    for s in range(2):
                        m = 2 * i + s
                        u = MT * f + m
                        n = MT * k + m
                        if odd:
                            with dve.If(many > 0):
                                dve.wait_ge(a_hi_used, n + 1)
                                dve.tensor_tensor(a_hi[:, s], at_block(m), a_hi[:, s].bitcast(F32),
                                                  ALU.subtract).then_inc(a_lo_ready, 1)
                        if not (last and s == 1):
                            stage_lo(dve, u + 1, odd, m + 1, 1 - s)
                        elif more and not new_h:
                            stage_lo(dve, u + 1, 1 - odd, 0, 0)
                        if more and not at_start:
                            split_w_lo(dve, f + 1, i - 1, s)
                        if beside and not last:
                            for r in range(BPT):
                                g = LATE + BPT * m + r
                                destination_hots(g, g)
                                if r > 0:
                                    add_window(g - 1, g - 1, (r - 1) % 2)
                            add_window(g, g, (BPT - 1) % 2)
                        if not odd:
                            evacuate_p(n, m, s)
                            continue
                        if l == 0:
                            wait(dve, h1t_turned, n - 1)
                            addend = bias[:]
                        else:
                            wait(dve, stored[s], 16 * (c * (MT // 2) + i))
                            dve.wait_ge(xres_ready, MT * c + m + 1)
                            addend = side[0:Q, s, :]
                        dve.wait_ge(tile_done, u + 1)
                        dve.tensor_tensor(tile_out[:, s, :], acc[s][:], addend, ALU.add).then_inc(out_ready, 1)

                pairs(dve, pair, 0, MT // 2 - 1)
                pair(MT // 2 - 1, last=True)
                if new_h:
                    stage_lo(dve, MT * (f + 1), 0, 0, 0)

            with dve.If(slow > 0):
                with dve.Fori(LATE // 2, NG // 2) as i:
                    for s in range(2):
                        destination_hots(2 * i + s, 2 * i + s)
                        add_window(2 * i + s, 2 * i + s, s)
                with dve.If(n_pass > 1):
                    with dve.Fori(1, n_pass) as ps:
                        dve.wait_ge(dst_hot_ready, 2 * NG * ps)
                        dve.tensor_scalar(key_t[:], key_t[:], -float(WIN), None, ALU.add).then_inc(pass_keys, 1)
                        dve.tensor_scalar(start_row[:], start_row[:], float(WIN), float(N * MT), ALU.add, ALU.min)\
                           .then_inc(pass_keys, 1)
                        dve.wait_ge(pass_keys, 3 * ps - 1)
                        dve.tensor_copy(start_int[:], start_row[:]).then_inc(pass_keys, 1)
                        with dve.Fori(0, NG // 2) as i:
                            dve.wait_ge(pass_keys, 3 * ps)
                            for s in range(2):
                                destination_hots(NG * ps + 2 * i + s, 2 * i + s)
                                add_window(NG * ps + 2 * i + s, 2 * i + s, s)
                dve.wait_ge(win_added, NG * n_pass)
                dve.sem_inc(a_ready, 1)
                phase(1)
            with dve.Else():
                phase(1, beside=True)
                dve.wait_ge(win_added, NG)
                dve.sem_inc(a_ready, 1)
            for f in range(2, len(phases)):
                phase(f)

        @block.tensor
        def _(pe):
            def count_half(n, s, h):
                pe.wait_ge(src_hot_ready, 2 * n + h + 1)
                pe.wait_ge(dst_hot_ready, 2 * n + h + 1)
                if h == 0:
                    wait(pe, win_added, n - 1)
                for j in range(HJ):
                    mm = pe.matmul(win[s][:, 0:WIN], src_hot[:, h, j, :], dst_hot[:, h, j, :],
                                   start=(h == 0 and j == 0), stop=(h == 1 and j == HJ - 1))
                mm.then_inc(hots_used, 1)

            def count_group(n, s):
                count_half(n, s, 0)
                count_half(n, s, 1)

            def times_weights(f, s, t, start, stop):
                w = w_hi[f % 2][:, t, :], w_lo[f % 2][:, t, :]
                pe.matmul(acc[s][:], lhs_hi[:, s, t, :], w[0], start=start, stop=False)
                pe.matmul(acc[s][:], lhs_hi[:, s, t, :], w[1], start=False, stop=False)
                return pe.matmul(acc[s][:], lhs_lo[:, s, t, :], w[0], start=False, stop=stop)

            pe.wait_ge(consts_ready, 3)
            pe.wait_ge(key_cols_ready, 1)
            for j in range(EJ):
                of_tile = slice(j * NG, (j + 1) * NG)
                for what, to in ((key, kp[0]), (negq, kp[1])):
                    pe.transpose(to[0:EP, of_tile], what[:].rearrange("g (p j) -> g j p", j=EJ)[:, j], ident[0:NG, 0:NG])
            for r, col in enumerate((COL_START, COL_END)):
                row = pe.transpose(kp[r][0:1, EJ * NG:(EJ + 1) * NG], group_col[:, col:col + 1], ident[0:NG, 0:NG])
            row.then_inc(keys_turned, 1)
            for m in range(MT):
                pe.wait_ge(xn_ready, m + 1)
                for s in range(2):
                    wait(pe, ht_ready, 2 * m + s - 1)
                    for t in range(KC):
                        col = (KC * s + t) * P
                        turned = pe.transpose(tp[s][:, t * Q:(t + 1) * Q], x_all[:, m, col:col + P], ident[0:Q, 0:Q])
                    turned.then_inc(xt_ready, 1)

            pe.wait_ge(rows_ready, 1)
            pe.wait_ge(keys_ready, 2)
            pe.matmul(kp[1][0:NG, 0:2 * NG], ones_row[:], rows[:].rearrange("o r g -> o (r g)"),
                      start=True, stop=True).then_inc(rows_spread, 1)

            def sum_overlaps():
                pe.wait_ge(overlap_ready, 1)
                pe.matmul(kp[0][0:1, 0:NG], group_col[:, COL_ONE:COL_ONE + 1], overlap[:, 1, :],
                          start=True, stop=True).then_inc(overlap_summed, 1)

            def phase(f, beside=False, many=None):
                l, c, odd = phases[f]
                k = CH * l + c

                def times_counts(s, halves=()):
                    for j in range(MT):
                        if j % 3 == 0 and j // 3 < len(halves):
                            count_half(*halves[j // 3])
                        for part in (p_hi, p_lo):
                            mm = pe.matmul(acc[s][:], a_hi[:, s, j, :], part[:, j, :], start=False, stop=False)
                    return mm

                def pair(i, last=False):
                    at_start = isinstance(i, int) and i == 0
                    for s in range(2):
                        m = 2 * i + s
                        u = MT * f + m
                        if at_start and s == 0:
                            pe.wait_ge(w_hi_ready, KT * (f + 1))
                            pe.wait_ge(w_lo_ready, KT * (f + 1))
                        if not at_start:
                            pe.wait_ge(out_ready if odd else p_lo_ready, MT * k + m - 1)
                        elif odd:
                            pe.wait_ge(p_lo_ready, MT * (k + 1) - 1 + s)
                        else:
                            wait(pe, out_ready, MT * k - 1 + s)
                        pe.wait_ge(lhs_hi_ready, u + 1)
                        pe.wait_ge(lhs_lo_ready, u + 1)
                        halves = []
                        if f == 0:
                            halves = [(g, r % 2, h) for r, g in enumerate(early_groups(i, s)) for h in range(2)]
                        for t in range(KT):
                            if halves and t % (KT // len(halves)) == 0:
                                count_half(*halves[t // (KT // len(halves))])
                            if t == KT - 1 and odd:
                                if at_start and s == 0:
                                    pe.wait_ge(p_lo_ready, MT * (k + 1))
                                pe.wait_ge(a_hi_ready, MT * k + m + 1)
                                late = []
                                if beside and not last:
                                    late = [(LATE + BPT * m + r, r % 2, h) for r in range(BPT) for h in range(2)]
                                times_counts(s, late).then_inc(a_hi_used, 1)
                                with pe.If(many > 0):
                                    pe.wait_ge(a_lo_ready, MT * k + m + 1)
                                    times_counts(s)
                            mm = times_weights(f, s, t, start=(t == 0), stop=(t == KT - 1))
                        mm.then_inc(tile_done, 1)
                        if l == 0 and odd and not (at_start and s == 0):
                            turn_h1(MT * c + m - 1, 1 - s)
                        if f == 0 and at_start and s == 0:
                            sum_overlaps()

                def turn_h1(n, s):
                    pe.wait_ge(out_ready, n + 1)
                    wait(pe, h1t_ready, n - 1)
                    for t in range(KC):
                        turned = pe.transpose(tp[s][:, t * Q:(t + 1) * Q], tile_out[:, s, t * P:(t + 1) * P],
                                              ident[0:Q, 0:Q])
                    turned.then_inc(h1t_turned, 1)

                pairs(pe, pair, 0, MT // 2 - 1)
                pair(MT // 2 - 1, last=True)
                if l == 0 and odd:
                    turn_h1(MT * c + MT - 1, 1)

            phase(0)
            pe.wait_ge(flags_ready, 1)
            n_pass = pe.value_load(flags[0:1, N_PASS:N_PASS + 1], min_val=1, max_val=N // WIN_D + 1)
            slow = pe.value_load(flags[0:1, SLOW:SLOW + 1], min_val=0, max_val=1)
            many = pe.value_load(flags[0:1, MANY:MANY + 1], min_val=0, max_val=1)
            with pe.If(slow > 0):
                with pe.Fori(LATE // 2, NG // 2) as i:
                    for s in range(2):
                        count_group(2 * i + s, s)
                with pe.If(n_pass > 1):
                    with pe.Fori(1, n_pass) as ps:
                        with pe.Fori(0, NG // 2) as i:
                            for s in range(2):
                                count_group(NG * ps + 2 * i + s, s)
                phase(1, many=many)
            with pe.Else():
                phase(1, beside=True, many=many)
            for f in range(2, len(phases)):
                phase(f, many=many)


_INS = ["x", "src", "dst", "L0_gnn_Ws1", "L0_gnn_Wn1", "L0_gnn_b1", "L0_gnn_Ws2", "L0_gnn_Wn2", "L0_gnn_b2"]


def kernel(**inputs):
    import numpy as _np
    import concourse.bacc as _bacc
    from concourse import mybir as _mybir
    from concourse.bass_utils import run_bass_kernel_spmd as _run

    nc = _bacc.Bacc("TRN2", target_bir_lowering=False, num_devices=1, dynamic_dma_scratch_size=1024)
    arrays, aps = {}, {}
    for name in _INS:
        a = _np.ascontiguousarray(inputs[name])
        arrays[f"in_{name}"] = a
        aps[name] = nc.dram_tensor(f"in_{name}", a.shape, _mybir.dt.from_np(a.dtype), kind="ExternalInput").ap()
    shape = arrays["in_x"].shape
    out = nc.dram_tensor("out_h", shape, _mybir.dt.float32, kind="ExternalOutput").ap()
    gnn_program(nc, aps["x"], aps["src"], aps["dst"], [aps["L0_gnn_Ws1"], aps["L0_gnn_Ws2"]],
                [aps["L0_gnn_Wn1"], aps["L0_gnn_Wn2"]], [aps["L0_gnn_b1"], aps["L0_gnn_b2"]], out)
    r = _run(nc, [arrays], core_ids=[0])
    return r.results[0]["out_h"]
```

```python
from contextlib import ExitStack

import concourse.bass as bass
from concourse import mybir

ALU = mybir.AluOpType
ACT = mybir.ActivationFunctionType
AX_X = mybir.AxisListType.X
F32 = mybir.dt.float32
F32R = mybir.dt.float32r
F16 = mybir.dt.float16
BF16 = mybir.dt.bfloat16
I32 = mybir.dt.int32
U32 = mybir.dt.uint32
U16 = mybir.dt.uint16

P = 128
EPS = 1e-5
ROUND = float(3 * 2 ** 22)


def gnn_program(nc, x, src, dst, Ws, Wn, b, out):
    N, D = x.shape
    E = src.shape[0]
    MT = 10
    Q = N // MT
    KT = D // P
    CH = 2
    CW = D // CH
    KC = CW // P
    EP = 125
    EJ = 4
    GE = EP * EJ
    NG = E // GE
    WIN_D = 20
    WIN = WIN_D * MT
    GPT = 4
    BPT, BT = 6, MT - 2
    LATE = NG - BPT * BT
    HS = 4
    BY_ACT = 2
    EXACT = 4096
    COL_START, COL_END, COL_ONE = 2, 3, 4
    N_PASS, SLOW, MANY = 0, 1, 2
    assert N == MT * Q and NG * GE == E and WIN <= 512 and Q <= P and MT % 2 == 0
    assert GPT * (MT - 2) == LATE and 2 * GPT % HS == 2 * BPT % HS == 0 and LATE % 2 == NG % 2 == 0

    def early_groups(i, s, behind=0):
        groups = [(2 * GPT * (i - 1) + g, g % HS, g % 2) for g in range(GPT * s - behind, GPT * (s + 1) - behind)]
        return [group for group in groups if group[0] >= 0] if isinstance(i, int) else groups

    def late_groups(i, s, behind=0):
        at = [LATE + BPT * s + r - behind for r in range(BPT)]
        return [(2 * BPT * i + g, g % HS, g % 2) for g in at]

    x_rows = x.rearrange("(q m) d -> q (m d)", m=MT)
    x_tiles = x.rearrange("(m r) d -> m r d", m=MT)
    out_tiles = out.rearrange("(m r) d -> m r d", m=MT)
    w_tiles = [[W.rearrange("(t p) n -> p t n", p=P) for W in pair] for pair in zip(Wn, Ws)]
    h1_spill = nc.dram_tensor("h1_spill", [MT, P, KC * Q], F32).ap()

    phases = [(l, c, odd) for l in range(2) for c in range(CH) for odd in range(2)]
    XP = MT // 2
    TURNED = {0: (2, 3), 1: (4, 5, 6), 2: (7, 8, 9)}

    with ExitStack() as ctx:
        def sb(name, shape, dt):
            return ctx.enter_context(nc.sbuf_tensor(name, shape, dt))

        def psum(name, shape, dt=F32):
            return ctx.enter_context(nc.psum_tensor(name, shape, dt))

        def sem(name):
            return ctx.enter_context(nc.semaphore(name))

        hT = sb("hT", [P, KT, N], F32)
        lhs_hi = sb("lhs_hi", [P, 2, KT, Q], F32R)
        lhs_lo = sb("lhs_lo", [P, 2, KT, Q], F32R)
        AT = sb("AT", [Q, N * MT + WIN], U16)
        w_raw = sb("w_raw", [P, 2, CW], F32)
        wn_hi = sb("wn_hi", [P, KT, CW], F32R)
        wn_lo = sb("wn_lo", [P, KT, CW], F32R)
        bias = sb("bias", [Q, CW], F32)
        ident = sb("ident", [P, P], F32)
        iota_w = sb("iota_w", [EP, WIN], F16)
        iota_q = sb("iota_q", [EP, Q], F16)
        iota_negq = sb("iota_negq", [EP, Q], F16)
        key_t = sb("key_t", [EP, NG, EJ], F32)
        negq_t = sb("negq_t", [EP, NG, EJ], F32)
        stats = sb("stats", [Q, MT, 2, 6], F32)
        mean_var = sb("mean_var", [Q, MT, 2], F32)
        rstd = sb("rstd", [Q, MT], F32)
        group_col = sb("group_col", [NG, 8], F32)
        start_row = sb("start_row", [1, NG], F32)
        start_int = sb("start_int", [1, NG], I32)
        rows = sb("rows", [1, 2, NG], F32)
        order_row = sb("order_row", [1, 2, NG], F32)
        row_f = sb("row_f", [1, 8], F32)
        ones_row = sb("ones_row", [1, NG], F32)
        overlap = sb("overlap", [NG, 2, NG], F32)
        flags = sb("flags", [1, 3], I32)

        with ExitStack() as early:
            def early_sb(name, shape, dt):
                return early.enter_context(nc.sbuf_tensor(name, shape, dt))

            x_all = early_sb("x_all", [Q, MT, D], F32)
            dst_i = early_sb("dst_i", [NG, GE], I32)
            src_i = early_sb("src_i", [NG, GE], I32)
            dst_f = early_sb("dst_f", [NG, GE], F32)
            src_f = early_sb("src_f", [NG, GE], F32)
            negq = early_sb("negq", [NG, GE], F32)
            key = early_sb("key", [NG, GE], F32)
            w_first = early_sb("w_first", [P, KT, CW], F32)
        p_split = sb("p_split", [Q, MT, 2, CW], F32R)
        p_hi, p_lo = p_split[:, :, 0, :], p_split[:, :, 1, :]
        ws_hi = sb("ws_hi", [P, KT, CW], F32R)
        ws_lo = sb("ws_lo", [P, KT, CW], F32R)
        a_hi = sb("a_hi", [Q, 2, MT, Q], F32R)
        tile_out = sb("tile_out", [P, 2, CW], F32)
        with ExitStack() as layer_0:
            dst_hot = layer_0.enter_context(nc.sbuf_tensor("dst_hot", [EP, HS, EJ, WIN], BF16))
            src_hot = layer_0.enter_context(nc.sbuf_tensor("src_hot", [EP, HS, EJ, Q], BF16))
        side = sb("side", [Q, 2, CW], F32)

        w_hi, w_lo = [wn_hi, ws_hi], [wn_lo, ws_lo]

        def node_tile(odd, m, t0=0, t1=KT):
            if odd:
                return hT[:, t0:t1, :].rearrange("p t (m r) -> p m t r", m=MT)[:, m]
            return hT[:, t0:t1, :].rearrange("p t (q m) -> p m t q", m=MT)[:, m]

        def at_block(m):
            return AT[:, 0:N * MT].rearrange("p (m r c) -> p m c r", m=MT, c=MT)[:, m]

        acc = [psum(f"acc{s}", [Q, CW]) for s in range(2)]
        win = [psum(f"win{s}", [Q, 512]) for s in range(2)]
        tp = [psum(f"tp{s}", [P, 512]) for s in range(2)]
        kp = [psum(f"kp{s}", [P, 512]) for s in range(2)]

        edges_loaded = sem("edges_loaded")
        x_loaded = [sem(f"x_loaded{i}") for i in range(XP)]
        bias_loaded = sem("bias_loaded")
        w_first_loaded = [sem(f"w_first_loaded{half}") for half in range(2)]
        w_raw_loaded = [sem(f"w_raw_loaded{s}") for s in range(2)]
        w_hi_ready = sem("w_hi_ready")
        w_lo_ready = sem("w_lo_ready")
        consts_ready = sem("consts_ready")
        at_zeroed = sem("at_zeroed")
        vec_step = sem("vec_step")
        key_cols_ready = sem("key_cols_ready")
        keys_turned = sem("keys_turned")
        keys_ready = sem("keys_ready")
        rows_ready = sem("rows_ready")
        rows_spread = sem("rows_spread")
        overlap_ready = sem("overlap_ready")
        overlap_summed = sem("overlap_summed")
        flags_ready = sem("flags_ready")
        var_ready = sem("var_ready")
        std_ready = sem("std_ready")
        xn_ready = sem("xn_ready")
        xt_ready = sem("xt_ready")
        ht_ready = sem("ht_ready")
        src_sq_ready = sem("src_sq_ready")
        src_hot_ready = sem("src_hot_ready")
        dst_hot_ready = sem("dst_hot_ready")
        hots_used = sem("hots_used")
        win_added = sem("win_added")
        pass_keys = sem("pass_keys")
        a_ready = sem("a_ready")
        lhs_hi_ready = sem("lhs_hi_ready")
        lhs_lo_ready = sem("lhs_lo_ready")
        first_hi_ready = sem("first_hi_ready")
        first_lo_ready = sem("first_lo_ready")
        tile_done = sem("tile_done")
        p_hi_ready = sem("p_hi_ready")
        p_lo_ready = sem("p_lo_ready")
        a_hi_ready = sem("a_hi_ready")
        a_hi_used = sem("a_hi_used")
        a_lo_ready = sem("a_lo_ready")
        out_ready = sem("out_ready")
        h1t_turned = sem("h1t_turned")
        h1t_ready = sem("h1t_ready")
        spilled = [sem(f"spilled{s}") for s in range(2)]
        reloaded = sem("reloaded")
        xres_loaded = [sem(f"xres_loaded{s}") for s in range(2)]
        xres_ready = sem("xres_ready")
        stored = [sem(f"stored{s}") for s in range(2)]

        def wait(eng, s, count):
            if not isinstance(count, int) or count > 0:
                eng.wait_ge(s, count)

        def pairs(eng, body, last=MT // 2, peel=1):
            for i in range(peel):
                body(i)
            with eng.Fori(peel, last) as i:
                body(i)

        block = ctx.enter_context(nc.Block())

        @block.sync
        def _(sp):
            def load_w(f, t, s):
                l, c, odd = phases[f]
                wait(sp, w_hi_ready, KT * f + t - 1)
                wait(sp, w_lo_ready, KT * f + t - 1)
                sp.dma_start(w_raw[:, s, :], w_tiles[l][odd][:, t, c * CW:(c + 1) * CW]).then_inc(w_raw_loaded[s], 16)

            sp.dma_start(dst_i[:], dst.rearrange("(g e) -> g e", g=NG)).then_inc(edges_loaded, 16)
            sp.dma_start(src_i[:], src.rearrange("(g e) -> g e", g=NG)).then_inc(edges_loaded, 16)
            for i in range(XP):
                sp.dma_start(x_all[:, 2 * i:2 * i + 2, :], x_rows[:, 2 * i * D:(2 * i + 2) * D])\
                  .then_inc(x_loaded[i], 16)
                if i < 2:
                    part = slice(i * KC, (i + 1) * KC)
                    sp.dma_start(w_first[:, part, :], w_tiles[0][0][:, part, 0:CW]).then_inc(w_first_loaded[i], 16)
            sp.dma_start(bias[:], b[0][0:CW].partition_broadcast(Q)).then_inc(bias_loaded, 16)

            for f, (l, c, odd) in enumerate(phases):
                chunk = slice(c * CW, (c + 1) * CW)
                k = CH * l + c
                if k > 0 and odd == 0:
                    sp.wait_ge(out_ready, MT * k)
                    sp.dma_start(bias[:], b[l][chunk].partition_broadcast(Q)).then_inc(bias_loaded, 16)
                if l == 1 and odd == 1:
                    sp.wait_ge(out_ready, MT * k)
                    for s in range(2):
                        sp.dma_start(side[:, s, :], x_tiles[s][:, chunk]).then_inc(xres_loaded[s], 16)

                def pair(i, last=False):
                    if f + 1 < len(phases) and not last:
                        for s in range(2):
                            load_w(f + 1, 2 * i + s, s)
                    if not odd:
                        return
                    for s in range(2):
                        m = 2 * i + s
                        if l == 0 and c == 0:
                            sp.wait_ge(h1t_ready, m + 1)
                            sp.dma_start(h1_spill[m], tile_out[:, s, 0:KC * Q]).then_inc(spilled[s], 16)
                        if l == 0 and c == 1:
                            sp.wait_ge(lhs_hi_ready, MT * f + m + 1)
                            sp.wait_ge(lhs_lo_ready, MT * f + m + 1)
                            sp.dma_start(node_tile(1, m, 0, KC), h1_spill[m].rearrange("p (t q) -> p t q", q=Q))\
                              .then_inc(reloaded, 16)
                        if l == 1:
                            sp.wait_ge(out_ready, MT * k + m + 1)
                            sp.dma_start(out_tiles[m][:, chunk], tile_out[0:Q, s, :]).then_inc(stored[s], 16)
                            if not last:
                                sp.dma_start(side[:, s, :], x_tiles[m + 2][:, chunk]).then_inc(xres_loaded[s], 16)

                if l == 0 and c == 1 and odd == 1:
                    for s in range(2):
                        sp.wait_ge(spilled[s], 16 * (MT // 2))
                if odd or f + 1 < len(phases):
                    pairs(sp, pair, MT // 2 - 1)
                    pair(MT // 2 - 1, last=True)
            for s in range(2):
                sp.wait_ge(stored[s], 16 * CH * (MT // 2))

        def load_flags(eng):
            eng.wait_ge(flags_ready, 1)
            return [eng.value_load(flags[0:1, n:n + 1], min_val=low, max_val=high)
                    for n, low, high in ((N_PASS, 1, N // WIN_D + 1), (SLOW, 0, 1), (MANY, 0, 1))]

        def split_w_lo(eng, f, n, s):
            t = 2 * n + s
            eng.wait_ge(w_hi_ready, KT * f + t + 1)
            raw = w_first[:, t, :] if f == 0 else w_raw[:, s, :]
            eng.tensor_tensor(w_lo[f % 2][:, t, :], raw, w_hi[f % 2][:, t, :].bitcast(F32),
                              ALU.subtract).then_inc(w_lo_ready, 1)

        def stage_lo(eng, u, odd, m, s, t0=0):
            eng.wait_ge(lhs_hi_ready, u + 1)
            eng.tensor_tensor(lhs_lo[:, s, t0:], node_tile(odd, m, t0), lhs_hi[:, s, t0:].bitcast(F32),
                              ALU.subtract).then_inc(lhs_lo_ready, 1)

        @block.gpsimd
        def _(pool):
            pool.memset(ident[:], 0.0).then_inc(consts_ready, 1)
            pool.memset(ones_row[:], 1.0).then_inc(consts_ready, 1)
            pool.wait_ge(consts_ready, 2)
            pool.affine_select(out=ident[:], in_=ident[:], compare_op=ALU.not_equal, fill=1.0, base=0,
                               pattern=[[-1, P]], channel_multiplier=1).then_inc(consts_ready, 1)
            pool.iota(iota_q[:], [[1, Q]], base=0, channel_multiplier=0,
                      allow_small_or_imprecise_dtypes=True).then_inc(consts_ready, 1)
            pool.iota(iota_negq[:], [[-1, Q]], base=0, channel_multiplier=0,
                      allow_small_or_imprecise_dtypes=True).then_inc(consts_ready, 1)
            pool.iota(iota_w[:], [[1, WIN]], base=0, channel_multiplier=0,
                      allow_small_or_imprecise_dtypes=True).then_inc(consts_ready, 1)
            pool.iota(order_row[:, 0, LATE - BPT:].rearrange("o (j r) -> o j r", r=BPT), [[Q * MT, BT + 1], [0, BPT]],
                      base=Q * MT, channel_multiplier=0,
                      allow_small_or_imprecise_dtypes=True).then_inc(consts_ready, 1)
            pool.memset(AT[:].bitcast(U32), 0).then_inc(at_zeroed, 1)
            for t in range(KT):
                split_w_lo(pool, 0, t // 2, t % 2)
            pool.wait_ge(lhs_lo_ready, 1)

            def pair(i, last=False):
                for s in range(2):
                    m = 2 * i + s
                    if last and s == 1:
                        stage_lo(pool, MT, 1, 0, 0)
                    else:
                        stage_lo(pool, m + 1, 0, m + 1, 1 - s)
                    if not (isinstance(i, int) and i == 0):
                        split_w_lo(pool, 1, i - 1, s)

            pairs(pool, pair, MT // 2 - 1)
            pair(MT // 2 - 1, last=True)

            for c in range(CH):
                pool.wait_ge(bias_loaded, 16 * (CH + c + 1))

                def add_bias(i):
                    for s in range(2):
                        pool.wait_ge(xres_loaded[s], 16 * (c * (MT // 2) + i + 1))
                        pool.tensor_tensor(side[:, s, :], side[:, s, :], bias[:], ALU.add).then_inc(xres_ready, 1)

                pairs(pool, add_bias)

        @block.scalar
        def _(act):
            def split_w_hi(f, n, s):
                if f == 0:
                    act.wait_ge(w_first_loaded[2 * n // KC], 16)
                    raw = w_first[:, 2 * n + s, :]
                else:
                    act.wait_ge(w_raw_loaded[s], 16 * (KT // 2 * (f - 1) + n + 1))
                    raw = w_raw[:, s, :]
                act.activation(w_hi[f % 2][:, 2 * n + s, :], raw, ACT.Copy).then_inc(w_hi_ready, 1)

            def stage_hi(u, odd, m, s, t0=0):
                wait(act, tile_done, u - 1)
                act.activation(lhs_hi[:, s, t0:], node_tile(odd, m, t0), ACT.Copy).then_inc(lhs_hi_ready, 1)

            def stage_a(n, u, m, s):
                wait(act, tile_done, u - 1)
                act.activation(a_hi[:, s], at_block(m), ACT.Copy).then_inc(a_hi_ready, 1)

            def evacuate_p(n, m, s):
                act.activation(p_hi[:, m, :], acc[s][:], ACT.Copy).then_inc(p_hi_ready, 1)

            def source_hots(n, g, h, ring=HS):
                wait(act, hots_used, n - ring + 1)
                for j in range(BY_ACT):
                    square = act.activation(src_hot[:, h, j, :], iota_q[:], ACT.Square, bias=negq_t[:, g, j:j + 1])
                square.then_inc(src_sq_ready, 1)
                act.wait_ge(src_sq_ready, n + 1)
                share = src_hot[:, h, 0:BY_ACT, :]
                act.activation(share, share, ACT.Relu, bias=1.0, scale=-1.0).then_inc(src_hot_ready, 1)

            def take_std(p):
                act.wait_ge(var_ready, p + 1)
                act.activation(rstd[:, 2 * p:2 * p + 2], rstd[:, 2 * p:2 * p + 2], ACT.Sqrt).then_inc(std_ready, 1)

            def evacuate_ht(m):
                for s in range(2):
                    act.wait_ge(xt_ready, 2 * m + s + 1)
                    act.activation(node_tile(0, m, KC * s, KC * (s + 1)),
                                   tp[s][:, 0:KC * Q].rearrange("p (t q) -> p t q", q=Q), ACT.Relu)\
                       .then_inc(ht_ready, 1)

            take_std(0)
            for t in range(4):
                split_w_hi(0, t // 2, t % 2)
            evacuate_ht(0)
            act.wait_ge(ht_ready, 2)
            stage_hi(0, 0, 0, 0)
            for t in range(4, KT):
                split_w_hi(0, t // 2, t % 2)
            evacuate_ht(1)
            take_std(1)
            act.wait_ge(consts_ready, 7)
            act.wait_ge(keys_ready, 2)

            def phase(f, beside=False):
                l, c, odd = phases[f]
                k = CH * l + c
                more = f + 1 < len(phases)

                def evacuate_h1t(n, m, s):
                    act.wait_ge(h1t_turned, n + 1)
                    turned = tp[s][:, 0:KC * Q]
                    if c == 0:
                        act.activation(tile_out[:, s, 0:KC * Q], turned, ACT.Copy).then_inc(h1t_ready, 1)
                    else:
                        act.activation(node_tile(1, m, KC, KT), turned.rearrange("p (t q) -> p t q", q=Q), ACT.Copy)\
                           .then_inc(h1t_ready, 1)

                new_h = (l, c, odd) == (0, CH - 1, 1)

                def pair(i, last=False):
                    at_start = isinstance(i, int) and i == 0
                    for s in range(2):
                        m = 2 * i + s
                        u = MT * f + m
                        groups = early_groups(i, s) if f == 0 and not at_start else []
                        if beside and not last:
                            groups = late_groups(i, s)
                        for g, h, w in groups[:1]:
                            source_hots(g, g, h)
                        if not odd and not (at_start and s == 0):
                            act.wait_ge(tile_done, u)
                            evacuate_p(MT * k + m - 1, m - 1, 1 - s)
                        if f == 0 and isinstance(i, int) and m <= 3:
                            for tile in TURNED.get(m - 1, ()):
                                evacuate_ht(tile)
                            act.wait_ge(ht_ready, 2 * (max(TURNED.get(m - 1, [1])) + 1))
                        if not (last and s == 1):
                            stage_hi(u + 1, odd, m + 1, 1 - s)
                        if f == 0 and isinstance(i, int) and m < 2:
                            for p in ((2,), (3, 4))[m]:
                                take_std(p)
                        for g, h, w in groups[1:3]:
                            source_hots(g, g, h)
                        if not (last and s == 1):
                            if odd:
                                if beside:
                                    act.wait_ge(win_added, LATE - BPT + BPT * (m + 1))
                                stage_a(MT * k + m + 1, u + 1, m + 1, 1 - s)
                        elif more and not new_h:
                            stage_hi(u + 1, 1 - odd, 0, 0)
                        for g, h, w in groups[3:]:
                            source_hots(g, g, h)
                        if more and not at_start:
                            split_w_hi(f + 1, i - 1, s)
                        if odd and l == 0 and not (at_start and s == 0):
                            evacuate_h1t(MT * c + m - 1, m - 1, 1 - s)

                if odd:
                    if beside:
                        act.wait_ge(win_added, LATE - BPT)
                    else:
                        act.wait_ge(a_ready, 1)
                    stage_a(MT * k, MT * f, 0, 0)
                pairs(act, pair, MT // 2 - 1, 1 + (f == 0))
                if f == 0:
                    loaded.extend(load_flags(act))
                pair(MT // 2 - 1, last=True)
                if not odd:
                    act.wait_ge(tile_done, MT * (f + 1))
                    evacuate_p(MT * k + MT - 1, MT - 1, 1)
                elif l == 0:
                    if new_h:
                        act.wait_ge(reloaded, 16 * MT)
                        act.wait_ge(tile_done, MT * (f + 1) - 1)
                        act.activation(lhs_hi[:, 0, 0:KC], node_tile(0, 0, 0, KC), ACT.Copy).then_inc(first_hi_ready, 1)
                    evacuate_h1t(MT * c + MT - 1, MT - 1, 1)
                    if new_h:
                        act.wait_ge(h1t_ready, MT * CH)
                        stage_hi(MT * (f + 1), 0, 0, 0, KC)

            loaded = []
            phase(0)
            n_pass, slow, many = loaded
            with act.If(slow > 0):
                with act.Fori(LATE // 2, NG // 2) as i:
                    for s in range(2):
                        source_hots(2 * i + s, 2 * i + s, s, 2)
                with act.If(n_pass > 1):
                    with act.Fori(1, n_pass) as ps:
                        with act.Fori(0, NG // 2) as i:
                            for s in range(2):
                                source_hots(NG * ps + 2 * i + s, 2 * i + s, s, 2)
                phase(1)
            with act.Else():
                phase(1, beside=True)
            for f in range(2, len(phases)):
                phase(f)

        @block.vector
        def _(dve):
            steps = [0]

            def step(instruction):
                steps[0] += 1
                instruction.then_inc(vec_step, 1)
                dve.wait_ge(vec_step, steps[0])

            def destination_hots(n, g, h, ring=HS):
                wait(dve, hots_used, n - ring + 1)
                for j in range(EJ):
                    if j >= BY_ACT:
                        dve.tensor_scalar(src_hot[:, h, j, :], iota_negq[:], negq_t[:, g, j:j + 1], None,
                                          ALU.is_equal)
                    hot = dve.tensor_scalar(dst_hot[:, h, j, :], iota_w[:], key_t[:, g, j:j + 1], None, ALU.is_equal)
                hot.then_inc(dst_hot_ready, 1)

            def window_starts(g, count=1):
                _, starts = nc.values_load_multi_w_load_instructions(
                    start_int[0:1, bass.ds(g, count)], engines=[mybir.EngineType.DVE], min_val=0, max_val=N * MT,
                    skip_runtime_bounds_check_because="starts are destinations times MT, at most N * MT")
                return starts

            def add_window(n, g, w, start=None):
                if start is None:
                    start, = window_starts(g)
                dve.wait_ge(hots_used, n + 1)
                wait(dve, win_added, n)
                dve.tensor_tensor(AT[:, bass.ds(start, WIN)], win[w][:, 0:WIN], AT[:, bass.ds(start, WIN)],
                                  ALU.add).then_inc(win_added, 1)

            def take_var(p):
                dve.wait_ge(x_loaded[p], 16)
                for m in (2 * p, 2 * p + 1):
                    for s in range(2):
                        stat = dve.bn_stats(stats[:, m, s, :], x_all[:, m, CW * s:CW * (s + 1)])
                step(stat)
                for m in (2 * p, 2 * p + 1):
                    stat = dve.bn_aggr(mean_var[:, m, :], stats[:, m])
                step(stat)
                dve.tensor_scalar(rstd[:, 2 * p:2 * p + 2], mean_var[:, 2 * p:2 * p + 2, 1], EPS, None, ALU.add)\
                   .then_inc(var_ready, 1)

            def normalise(p):
                dve.wait_ge(std_ready, p + 1)
                step(dve.reciprocal(rstd[:, 2 * p:2 * p + 2], rstd[:, 2 * p:2 * p + 2]))
                for m in (2 * p, 2 * p + 1):
                    dve.tensor_scalar(x_all[:, m, :], x_all[:, m, :], mean_var[:, m, 0:1], rstd[:, m:m + 1],
                                      ALU.subtract, ALU.mult).then_inc(xn_ready, 1)

            dve.wait_ge(edges_loaded, 32)
            dve.tensor_copy(dst_f[:], dst_i[:])
            step(dve.tensor_copy(src_f[:], src_i[:]))
            step(dve.tensor_scalar(negq[:], src_f[:], 1.0 / MT, -0.45, ALU.mult, ALU.add))
            dve.tensor_reduce(group_col[:, 0:1], dst_f[:], AX_X, ALU.min)
            step(dve.tensor_scalar(negq[:], negq[:], ROUND, None, ALU.add))
            dve.tensor_reduce(group_col[:, 1:2], dst_f[:], AX_X, ALU.max)
            step(dve.tensor_scalar(negq[:], negq[:], -ROUND, -1.0, ALU.add, ALU.mult))
            take_var(0)
            dve.tensor_scalar(group_col[:, COL_START:COL_START + 1], group_col[:, 0:1], float(MT), None, ALU.mult)
            dve.tensor_scalar(group_col[:, COL_END:COL_END + 1], group_col[:, 1:2], float(MT), None, ALU.mult)
            dve.memset(group_col[:, COL_ONE:COL_ONE + 1], 1.0)
            step(dve.scalar_tensor_tensor(out=key[:], in0=negq[:], scalar=float(MT), in1=src_f[:],
                                          op0=ALU.mult, op1=ALU.add))
            normalise(0)
            step(dve.scalar_tensor_tensor(out=key[:], in0=dst_f[:], scalar=float(MT), in1=key[:],
                                          op0=ALU.mult, op1=ALU.add))
            dve.tensor_scalar(key[:], key[:], group_col[:, COL_START:COL_START + 1], None,
                              ALU.subtract).then_inc(key_cols_ready, 1)
            take_var(1)
            stage_lo(dve, 0, 0, 0, 0)
            dve.wait_ge(keys_turned, 1)
            for to, bank in ((key_t, kp[0]), (negq_t, kp[1])):
                turned = bank[0:EP, 0:EJ * NG].rearrange("p (j g) -> p g j", j=EJ)
                dve.tensor_copy(to[:], turned).then_inc(keys_ready, 1)
            first_row, second_row = (kp[r][0:1, EJ * NG:(EJ + 1) * NG] for r in range(2))
            dve.tensor_copy(start_row[:], first_row)
            dve.tensor_copy(start_int[:], first_row)
            dve.tensor_copy(rows[:, 0, :], first_row)
            dve.tensor_copy(rows[:, 1, :], second_row).then_inc(rows_ready, 1)
            take_var(2)
            normalise(1)
            take_var(3)
            normalise(2)
            take_var(4)
            normalise(3)
            normalise(4)
            dve.wait_ge(consts_ready, 7)
            dve.wait_ge(keys_ready, 2)

            def set_flags():
                dve.wait_ge(rows_ready, 1)
                step(dve.tensor_tensor(order_row[:, 1, :], rows[:, 1, :], rows[:, 0, :], ALU.subtract))
                step(dve.tensor_reduce(row_f[:, 0:1], order_row[:, 1, :], AX_X, ALU.max))
                step(dve.tensor_scalar(row_f[:, 0:1], row_f[:, 0:1], 1.0 / WIN, 0.5 / WIN_D - 0.5, ALU.mult, ALU.add))
                step(dve.tensor_scalar(row_f[:, 0:1], row_f[:, 0:1], ROUND, None, ALU.add))
                step(dve.tensor_scalar(row_f[:, 0:1], row_f[:, 0:1], -ROUND, 1.0, ALU.add, ALU.add))
                dve.tensor_copy(flags[:, N_PASS:N_PASS + 1], row_f[:, 0:1])
                step(dve.tensor_tensor(order_row[:, 1, LATE - BPT:], rows[:, 0, LATE - BPT:],
                                       order_row[:, 0, LATE - BPT:], ALU.is_ge))
                step(dve.tensor_reduce(row_f[:, 1:2], order_row[:, 1, LATE - BPT:], AX_X, ALU.min))
                step(dve.tensor_scalar(row_f[:, 2:3], row_f[:, 0:1], 1.5, row_f[:, 1:2], ALU.is_lt, ALU.mult))
                step(dve.tensor_scalar(flags[:, SLOW:SLOW + 1], row_f[:, 2:3], -1.0, 1.0, ALU.mult, ALU.add))
                dve.wait_ge(rows_spread, 1)
                spread = kp[1][0:NG, 0:2 * NG]
                step(dve.tensor_scalar(overlap[:, 0, :], spread[:, 0:NG], group_col[:, COL_END:COL_END + 1], None,
                                       ALU.is_le))
                dve.scalar_tensor_tensor(out=overlap[:, 1, :], in0=spread[:, NG:2 * NG],
                                         scalar=group_col[:, COL_START:COL_START + 1], in1=overlap[:, 0, :],
                                         op0=ALU.is_ge, op1=ALU.mult).then_inc(overlap_ready, 1)

            def set_many():
                dve.wait_ge(overlap_summed, 1)
                step(dve.tensor_reduce(row_f[:, 3:4], kp[0][0:1, 0:NG], AX_X, ALU.max))
                dve.tensor_scalar(flags[:, MANY:MANY + 1], row_f[:, 3:4], float(EXACT // GE), None,
                                  ALU.is_gt).then_inc(flags_ready, 1)

            def evacuate_p(n, m, s):
                dve.wait_ge(p_hi_ready, n + 1)
                dve.tensor_tensor(p_lo[:, m, :], acc[s][:], p_hi[:, m, :].bitcast(F32),
                                  ALU.subtract).then_inc(p_lo_ready, 1)

            def edge_pair(i):
                at_start = isinstance(i, int) and i == 0
                for s in range(2):
                    m = 2 * i + s
                    for r, (g, h, w) in enumerate([] if at_start else early_groups(i, s)):
                        destination_hots(g, g, h)
                        if r == 0:
                            ahead = 0 if isinstance(g, int) and g < 2 else 2
                            starts = window_starts(g - ahead, GPT)
                        if not (isinstance(g, int) and g < 2):
                            add_window(g - 2, g - 2, w, starts[r - 2 + ahead])
                        if r == 0:
                            evacuate_p(m - 1, m - 1, 1 - s)
                        if isinstance(i, int) and (i, s, r) == (1, 1, 0):
                            set_flags()
                    if at_start and s == 1:
                        evacuate_p(0, 0, 0)
                    if isinstance(i, int) and (i, s) == (1, 1):
                        set_many()

            dve.wait_ge(at_zeroed, 1)
            pairs(dve, edge_pair, MT // 2 - 1, 2)
            n_pass, slow, many = load_flags(dve)
            edge_pair(MT // 2 - 1)
            evacuate_p(MT - 1, MT - 1, 1)

            dve.wait_ge(lhs_lo_ready, MT + 1)
            dve.wait_ge(w_lo_ready, 2 * KT)

            def phase(f, beside=False):
                l, c, odd = phases[f]
                k = CH * l + c
                more = f + 1 < len(phases)
                new_h = (l, c, odd) == (0, CH - 1, 1)
                if l == 0 and odd:
                    dve.wait_ge(bias_loaded, 16 * (c + 1))

                def finish(i, s):
                    m = 2 * i + s
                    if not odd:
                        evacuate_p(MT * k + m, m, s)
                        return
                    if l == 0:
                        wait(dve, h1t_turned, MT * k + m - 1)
                        wait(dve, spilled[s], 16 * i if c == 0 else 8 * MT)
                        addend = bias[:]
                    else:
                        wait(dve, stored[s], 16 * (c * (MT // 2) + i))
                        dve.wait_ge(xres_ready, MT * c + m + 1)
                        addend = side[:, s, :]
                    dve.wait_ge(tile_done, MT * f + m + 1)
                    dve.tensor_tensor(tile_out[0:Q, s, :], acc[s][:], addend, ALU.add).then_inc(out_ready, 1)

                def pair(i, last=False):
                    at_start = isinstance(i, int) and i == 0
                    for s in range(2):
                        m = 2 * i + s
                        u = MT * f + m
                        n = MT * k + m
                        late = late_groups(i, s) if beside and not last else []
                        for g, h, w in late[:1]:
                            destination_hots(g, g, h)
                            starts = window_starts(g - 2, BPT)
                        if s == 1:
                            finish(i, 0)
                        elif not at_start:
                            finish(i - 1, 1)
                        for g, h, w in late[:1]:
                            add_window(g - 2, g - 2, w, starts[0])
                        if odd:
                            with dve.If(many > 0):
                                dve.wait_ge(a_hi_used, n + 1)
                                dve.tensor_tensor(a_hi[:, s], at_block(m), a_hi[:, s].bitcast(F32),
                                                  ALU.subtract).then_inc(a_lo_ready, 1)
                        if not (last and s == 1):
                            stage_lo(dve, u + 1, odd, m + 1, 1 - s)
                        elif more and not new_h:
                            stage_lo(dve, u + 1, 1 - odd, 0, 0)
                        for r, (g, h, w) in enumerate(late[1:], 1):
                            destination_hots(g, g, h)
                            add_window(g - 2, g - 2, w, starts[r])
                        if beside and last and s == 0:
                            add_window(NG - 2, NG - 2, 0)
                            add_window(NG - 1, NG - 1, 1)
                        if more and not at_start:
                            split_w_lo(dve, f + 1, i - 1, s)

                pairs(dve, pair, MT // 2 - 1)
                pair(MT // 2 - 1, last=True)
                if new_h:
                    dve.wait_ge(first_hi_ready, 1)
                    dve.tensor_tensor(lhs_lo[:, 0, 0:KC], node_tile(0, 0, 0, KC), lhs_hi[:, 0, 0:KC].bitcast(F32),
                                      ALU.subtract).then_inc(first_lo_ready, 1)
                finish(MT // 2 - 1, 1)
                if new_h:
                    stage_lo(dve, MT * (f + 1), 0, 0, 0, KC)

            with dve.If(slow > 0):
                add_window(LATE - 2, LATE - 2, 0)
                add_window(LATE - 1, LATE - 1, 1)
                with dve.Fori(LATE // 2, NG // 2) as i:
                    for s in range(2):
                        destination_hots(2 * i + s, 2 * i + s, s, 2)
                        add_window(2 * i + s, 2 * i + s, s)
                with dve.If(n_pass > 1):
                    with dve.Fori(1, n_pass) as ps:
                        dve.wait_ge(dst_hot_ready, NG * ps)
                        dve.tensor_scalar(key_t[:], key_t[:], -float(WIN), None, ALU.add).then_inc(pass_keys, 1)
                        dve.tensor_scalar(start_row[:], start_row[:], float(WIN), float(N * MT), ALU.add, ALU.min)\
                           .then_inc(pass_keys, 1)
                        dve.wait_ge(pass_keys, 3 * ps - 1)
                        dve.tensor_copy(start_int[:], start_row[:]).then_inc(pass_keys, 1)
                        with dve.Fori(0, NG // 2) as i:
                            dve.wait_ge(pass_keys, 3 * ps)
                            for s in range(2):
                                destination_hots(NG * ps + 2 * i + s, 2 * i + s, s, 2)
                                add_window(NG * ps + 2 * i + s, 2 * i + s, s)
                dve.wait_ge(win_added, NG * n_pass)
                dve.sem_inc(a_ready, 1)
                phase(1)
            with dve.Else():
                phase(1, beside=True)
                dve.wait_ge(win_added, NG)
                dve.sem_inc(a_ready, 1)
            for f in range(2, len(phases)):
                phase(f)

        @block.tensor
        def _(pe):
            def count_group(n, h, w):
                pe.wait_ge(src_hot_ready, n + 1)
                pe.wait_ge(dst_hot_ready, n + 1)
                wait(pe, win_added, n - 1)
                for j in range(EJ):
                    mm = pe.matmul(win[w][:, 0:WIN], src_hot[:, h, j, :], dst_hot[:, h, j, :],
                                   start=(j == 0), stop=(j == EJ - 1))
                mm.then_inc(hots_used, 1)

            def times_weights(f, s, t, start, stop):
                w = w_hi[f % 2][:, t, :], w_lo[f % 2][:, t, :]
                pe.matmul(acc[s][:], lhs_hi[:, s, t, :], w[0], start=start, stop=False)
                pe.matmul(acc[s][:], lhs_hi[:, s, t, :], w[1], start=False, stop=False)
                return pe.matmul(acc[s][:], lhs_lo[:, s, t, :], w[0], start=False, stop=stop)

            pe.wait_ge(consts_ready, 3)

            def turn_x(m):
                pe.wait_ge(xn_ready, m + 1)
                for s in range(2):
                    wait(pe, ht_ready, 2 * m + s - 1)
                    for t in range(KC):
                        col = (KC * s + t) * P
                        turned = pe.transpose(tp[s][:, t * Q:(t + 1) * Q], x_all[:, m, col:col + P], ident[0:Q, 0:Q])
                    turned.then_inc(xt_ready, 1)

            turn_x(0)
            pe.wait_ge(key_cols_ready, 1)
            for j in range(EJ):
                of_tile = slice(j * NG, (j + 1) * NG)
                for what, to in ((key, kp[0]), (negq, kp[1])):
                    columns = what[:].rearrange("g (p j) -> g j p", j=EJ)[:, j]
                    pe.transpose(to[0:EP, of_tile], columns, ident[0:NG, 0:NG])
            for r, col in enumerate((COL_START, COL_END)):
                row = pe.transpose(kp[r][0:1, EJ * NG:(EJ + 1) * NG], group_col[:, col:col + 1], ident[0:NG, 0:NG])
            row.then_inc(keys_turned, 1)
            turn_x(1)

            def spread_rows():
                pe.wait_ge(rows_ready, 1)
                pe.wait_ge(keys_ready, 2)
                pe.matmul(kp[1][0:NG, 0:2 * NG], ones_row[:], rows[:].rearrange("o r g -> o (r g)"),
                          start=True, stop=True).then_inc(rows_spread, 1)

            def sum_overlaps():
                pe.wait_ge(overlap_ready, 1)
                pe.matmul(kp[0][0:1, 0:NG], group_col[:, COL_ONE:COL_ONE + 1], overlap[:, 1, :],
                          start=True, stop=True).then_inc(overlap_summed, 1)

            def phase(f, beside=False, many=None):
                l, c, odd = phases[f]
                k = CH * l + c

                def count_beside(groups, step, steps):
                    for r, group in enumerate(groups):
                        if r * steps // len(groups) == step:
                            count_group(*group)

                def times_counts(s, late=()):
                    for j in range(MT):
                        count_beside(late, KT - 1 + j, KT + MT)
                        for part in (p_hi, p_lo):
                            mm = pe.matmul(acc[s][:], a_hi[:, s, j, :], part[:, j, :], start=False, stop=False)
                    return mm

                def pair(i, last=False):
                    at_start = isinstance(i, int) and i == 0
                    for s in range(2):
                        m = 2 * i + s
                        u = MT * f + m
                        if not at_start:
                            pe.wait_ge(out_ready if odd else p_lo_ready, MT * k + m - 1)
                        elif odd:
                            pe.wait_ge(p_lo_ready, MT * (k + 1) - 1 + s)
                        else:
                            wait(pe, out_ready, MT * k - 1 + s)
                        from_halves = (l, c, odd) == (1, 0, 0) and at_start and s == 0
                        if from_halves:
                            pe.wait_ge(first_hi_ready, 1)
                            pe.wait_ge(first_lo_ready, 1)
                        else:
                            pe.wait_ge(lhs_hi_ready, u + 1)
                            pe.wait_ge(lhs_lo_ready, u + 1)
                        late = ()
                        if beside and not last:
                            late = late_groups(i, s, 1)
                        elif beside and s == 0:
                            late = (NG - 1, (NG - 1) % HS, 1),
                        for t in range(KT):
                            if f in (2, 4) and at_start and s == 0 and t == 1:
                                turn_h1(MT * k - 1, 1)
                            if from_halves and t == KC:
                                pe.wait_ge(lhs_hi_ready, u + 1)
                                pe.wait_ge(lhs_lo_ready, u + 1)
                            if at_start and s == 0:
                                pe.wait_ge(w_hi_ready, KT * f + t + 1)
                                pe.wait_ge(w_lo_ready, KT * f + t + 1)
                            if f == 0 and not at_start:
                                count_beside(early_groups(i, s, 1), t, KT)
                            elif t < KT - 1:
                                count_beside(late, t, KT + MT)
                            if t == KT - 1 and odd:
                                if l == 0 and not (at_start and s == 0):
                                    turn_h1(MT * c + m - 1, 1 - s)
                                if at_start and s == 0:
                                    pe.wait_ge(p_lo_ready, MT * (k + 1))
                                pe.wait_ge(a_hi_ready, MT * k + m + 1)
                                times_counts(s, late).then_inc(a_hi_used, 1)
                                with pe.If(many > 0):
                                    pe.wait_ge(a_lo_ready, MT * k + m + 1)
                                    times_counts(s)
                            if f == 0 and isinstance(i, int) and (m, t) == (3, KT - 2):
                                sum_overlaps()
                            mm = times_weights(f, s, t, start=(t == 0), stop=(t == KT - 1))
                        mm.then_inc(tile_done, 1)
                        if f == 0 and isinstance(i, int):
                            for tile in TURNED.get(m, ()):
                                turn_x(tile)
                            if m == 1:
                                spread_rows()

                def turn_h1(n, s):
                    pe.wait_ge(out_ready, n + 1)
                    wait(pe, h1t_ready, n - 1)
                    for t in range(KC):
                        turned = pe.transpose(tp[s][:, t * Q:(t + 1) * Q], tile_out[0:Q, s, t * P:(t + 1) * P],
                                              ident[0:Q, 0:Q])
                    turned.then_inc(h1t_turned, 1)

                pairs(pe, pair, MT // 2 - 1, 1 + (f == 0))
                if f == 0:
                    loaded.extend(load_flags(pe))
                pair(MT // 2 - 1, last=True)

            loaded = []
            phase(0)
            n_pass, slow, many = loaded
            with pe.If(slow > 0):
                count_group(LATE - 1, (LATE - 1) % HS, 1)
                with pe.Fori(LATE // 2, NG // 2) as i:
                    for s in range(2):
                        count_group(2 * i + s, s, s)
                with pe.If(n_pass > 1):
                    with pe.Fori(1, n_pass) as ps:
                        with pe.Fori(0, NG // 2) as i:
                            for s in range(2):
                                count_group(NG * ps + 2 * i + s, s, s)
                phase(1, many=many)
            with pe.Else():
                phase(1, beside=True, many=many)
            for f in range(2, len(phases)):
                phase(f, many=many)


_INS = ["x", "src", "dst", "L0_gnn_Ws1", "L0_gnn_Wn1", "L0_gnn_b1", "L0_gnn_Ws2", "L0_gnn_Wn2", "L0_gnn_b2"]


def kernel(**inputs):
    import numpy as _np
    import concourse.bacc as _bacc
    from concourse import mybir as _mybir
    from concourse.bass_utils import run_bass_kernel_spmd as _run

    nc = _bacc.Bacc("TRN2", target_bir_lowering=False, num_devices=1, dynamic_dma_scratch_size=1024)
    arrays, aps = {}, {}
    for name in _INS:
        a = _np.ascontiguousarray(inputs[name])
        arrays[f"in_{name}"] = a
        aps[name] = nc.dram_tensor(f"in_{name}", a.shape, _mybir.dt.from_np(a.dtype), kind="ExternalInput").ap()
    shape = arrays["in_x"].shape
    out = nc.dram_tensor("out_h", shape, _mybir.dt.float32, kind="ExternalOutput").ap()
    gnn_program(nc, aps["x"], aps["src"], aps["dst"], [aps["L0_gnn_Ws1"], aps["L0_gnn_Ws2"]],
                [aps["L0_gnn_Wn1"], aps["L0_gnn_Wn2"]], [aps["L0_gnn_b1"], aps["L0_gnn_b2"]], out)
    r = _run(nc, [arrays], core_ids=[0])
    return r.results[0]["out_h"]
```
